# Optimizing a Trainium2 kernel written in Bass

```python
import numpy as np
import jax
import jax.numpy as jnp

def _softmax(x, axis=-1):
    return jax.nn.softmax(x, axis=axis)

def _gelu(x):
    return jax.nn.gelu(x, approximate=True)

def _silu(x):
    return jax.nn.silu(x)

def _sigmoid(x):
    return jax.nn.sigmoid(x)

def _layernorm(x, axis=-1, eps=1e-05):
    m = jnp.mean(x, axis=axis, keepdims=True)
    v = jnp.var(x, axis=axis, keepdims=True)
    return (x - m) / jnp.sqrt(v + eps)

def _scatter_add(tgt, idx, src, axis=0):
    return tgt.at[idx].add(src)

def _segment_sum(src, seg, n):
    return jax.ops.segment_sum(src, seg, n)
kernel_name = 'mk_xattn_seq_d2_seqx_r8_95a116'

def setup_inputs(seed: int=0):
    np.random.seed(seed)
    _w = jnp.asarray

    def _rec_inputs():
        import jax
        import jax.numpy as jnp
        _rk = jax.random.key(seed)
        x = -0.0002928 + 1 * jax.random.normal(jax.random.fold_in(_rk, 1), (64, 64, 256), jnp.float32)
        _lenS = 64 - jax.random.randint(jax.random.fold_in(_rk, 7), (64,), 0, max(1, 64 // 4) + 1, jnp.int32)
        _lenS2 = 64 - jax.random.randint(jax.random.fold_in(_rk, 8), (64,), 0, max(1, 64 // 4) + 1, jnp.int32)
        _ctx_2048P = jax.random.normal(jax.random.fold_in(_rk, 11), (64, 16, 256), jnp.float32)
        _ctx_2048c = jax.random.dirichlet(jax.random.fold_in(_rk, 511), 0.3 * jnp.ones((16,), jnp.float32), (64, 64))
        _ctx_2048t = jnp.einsum('bsk,bkd->bsd', _ctx_2048c, _ctx_2048P)
        _ctx_2048t = _ctx_2048t * jax.lax.rsqrt(jnp.mean(jnp.square(_ctx_2048t)) + 1e-12) * 0.953939
        ctx_2048 = -1.39393e-06 + 0.999914 * (_ctx_2048t + 0.3 * jax.random.normal(jax.random.fold_in(_rk, 611), (64, 64, 256), jnp.float32))
        _validS = jnp.arange(64)[None, :] < _lenS[:, None]
        _validS2 = jnp.arange(64)[None, :] < _lenS2[:, None]
        _causal = jnp.tril(jnp.ones((64, 64), dtype=bool))
        mask_1x1xSxS2_fc1 = jnp.where(jnp.broadcast_to(_validS2[0:1, None, None, :], (1, 1, 64, 64)), 1.0, 0.0).astype(jnp.float32)
        mask_Bx1xSxS2_ff1 = jnp.where(jnp.ones((64, 1, 64, 64), dtype=bool), 1.0, 0.0).astype(jnp.float32)
        mask_Bx1xSxS2_ff0 = jnp.where(jnp.ones((64, 1, 64, 64), dtype=bool), 0.0, -1000000000.0).astype(jnp.float32)
        return (x, ctx_2048, mask_1x1xSxS2_fc1, mask_Bx1xSxS2_ff1, mask_Bx1xSxS2_ff0)
    x, ctx_2048, mask_1x1xSxS2_fc1, mask_Bx1xSxS2_ff1, mask_Bx1xSxS2_ff0 = _rec_inputs()

    def _L0_xattn_setup():
        import jax, jax.numpy as jnp
        import numpy as np
        H = 256
        NH = 16
        HD = H // NH
        EPS = 1e-05

        def gelu(x):
            return 0.5 * x * (1.0 + jnp.tanh(0.7978845608028654 * x * (1.0 + 0.044715 * x * x)))

        def layernorm(x, scale, bias):
            m = jnp.mean(x, axis=-1, keepdims=True)
            v = jnp.mean(jnp.square(x - m), axis=-1, keepdims=True)
            return (x - m) * jax.lax.rsqrt(v + EPS) * scale + bias

        def split_heads(x):
            b, s, _ = x.shape
            return x.reshape(b, s, NH, HD).transpose(0, 2, 1, 3)

        def merge_heads(x):
            b, nh, s, hd = x.shape
            return x.transpose(0, 2, 1, 3).reshape(b, s, nh * hd)

        def attention(q, k, v, mask):
            scores = jnp.einsum('bhqd,bhkd->bhqk', q, k) / jnp.sqrt(jnp.float32(HD))
            scores = scores * mask - 10000.0 * (1.0 - mask)
            probs = jax.nn.softmax(scores, axis=-1)
            return jnp.einsum('bhqk,bhkd->bhqd', probs, v)
        key = jax.random.key(seed)
        ks = jax.random.split(key, 16)
        b, s, t = (2, 128, 128)
        w = lambda k, i, o: jax.random.normal(k, (i, o), jnp.float32) * 0.02
        inp = {'hidden_states': jax.random.normal(ks[0], (b, s, H), jnp.float32), 'encoder_states': jax.random.normal(ks[1], (b, t, H), jnp.float32), 'ltor_mask': jnp.tril(jnp.ones((1, 1, s, s), jnp.float32)), 'cross_mask': jnp.ones((b, 1, s, t), jnp.float32), 'ln1_s': jnp.ones((H,), jnp.float32), 'ln1_b': jnp.zeros((H,), jnp.float32), 'w_qkv': w(ks[2], H, 3 * H), 'b_qkv': jnp.zeros((3 * H,), jnp.float32), 'w_ao': w(ks[3], H, H), 'b_ao': jnp.zeros((H,), jnp.float32), 'ln2_s': jnp.ones((H,), jnp.float32), 'ln2_b': jnp.zeros((H,), jnp.float32), 'w_q': w(ks[4], H, H), 'b_q': jnp.zeros((H,), jnp.float32), 'w_kv': w(ks[5], H, 2 * H), 'b_kv': jnp.zeros((2 * H,), jnp.float32), 'w_co': w(ks[6], H, H), 'b_co': jnp.zeros((H,), jnp.float32), 'ln3_s': jnp.ones((H,), jnp.float32), 'ln3_b': jnp.zeros((H,), jnp.float32), 'w1': w(ks[7], H, 4 * H), 'b1': jnp.zeros((4 * H,), jnp.float32), 'w2': w(ks[8], 4 * H, H), 'b2': jnp.zeros((H,), jnp.float32)}
        return inp
    _L0_xattn_all = _L0_xattn_setup()
    _L0_xattn_in = {k: v for k, v in _L0_xattn_all.items() if k in ('ln1_s', 'ln1_b', 'w_qkv', 'b_qkv', 'w_ao', 'b_ao', 'ln2_s', 'ln2_b', 'w_q', 'b_q', 'w_kv', 'b_kv', 'w_co', 'b_co', 'ln3_s', 'ln3_b', 'w1', 'b1', 'w2', 'b2')}
    del _L0_xattn_all

    def _L1_xattn_setup():
        import jax, jax.numpy as jnp
        import numpy as np
        H = 256
        NH = 32
        KVH = 8
        HD = H // NH
        GROUPS = NH // KVH
        EPS = 1e-06
        B, L, S = (4, 128, 128)

        def _gqa_forward(hidden_state, encoder_hidden_state, encoder_attention_mask, Wq, bq, Wk, bk, Wv, bv, Wo, bo, gamma, beta):
            b, l, _ = hidden_state.shape
            s = encoder_hidden_state.shape[1]
            q = hidden_state @ Wq + bq
            k = encoder_hidden_state @ Wk + bk
            v = encoder_hidden_state @ Wv + bv
            q = q.reshape(b, l, KVH, GROUPS, HD).transpose(0, 2, 3, 1, 4)
            k = k.reshape(b, s, KVH, HD).transpose(0, 2, 1, 3)
            v = v.reshape(b, s, KVH, HD).transpose(0, 2, 1, 3)
            scale = 1.0 / jnp.sqrt(jnp.asarray(HD, q.dtype))
            scores = jnp.einsum('bkgld,bksd->bkgls', q, k) * scale
            scores = scores + encoder_attention_mask[:, :, None, :, :]
            attn = jax.nn.softmax(scores, axis=-1)
            out = jnp.einsum('bkgls,bksd->bkgld', attn, v)
            out = out.transpose(0, 3, 1, 2, 4).reshape(b, l, H)
            out = out @ Wo + bo
            x = out + hidden_state
            mu = jnp.mean(x, axis=-1, keepdims=True)
            var = jnp.var(x, axis=-1, keepdims=True)
            return (x - mu) * jax.lax.rsqrt(var + EPS) * gamma + beta
        key = jax.random.key(seed)
        ks = jax.random.split(key, 12)
        sd = 0.02
        return {'hidden_state': jax.random.normal(ks[0], (B, L, H), jnp.float32), 'encoder_hidden_state': jax.random.normal(ks[1], (B, S, H), jnp.float32), 'encoder_attention_mask': jnp.zeros((B, 1, L, S), jnp.float32), 'Wq': jax.random.normal(ks[2], (H, H), jnp.float32) * sd, 'bq': jnp.zeros((H,), jnp.float32), 'Wk': jax.random.normal(ks[3], (H, KVH * HD), jnp.float32) * sd, 'bk': jnp.zeros((KVH * HD,), jnp.float32), 'Wv': jax.random.normal(ks[4], (H, KVH * HD), jnp.float32) * sd, 'bv': jnp.zeros((KVH * HD,), jnp.float32), 'Wo': jax.random.normal(ks[5], (H, H), jnp.float32) * sd, 'bo': jnp.zeros((H,), jnp.float32), 'gamma': jnp.ones((H,), jnp.float32), 'beta': jnp.zeros((H,), jnp.float32)}
    _L1_xattn_all = _L1_xattn_setup()
    _L1_xattn_in = {k: v for k, v in _L1_xattn_all.items() if k in ('Wq', 'bq', 'Wk', 'bk', 'Wv', 'bv', 'Wo', 'bo', 'gamma', 'beta')}
    del _L1_xattn_all
    return {'x': x, 'ctx_2048': ctx_2048, 'mask_1x1xSxS2_fc1': mask_1x1xSxS2_fc1, 'mask_Bx1xSxS2_ff1': mask_Bx1xSxS2_ff1, 'mask_Bx1xSxS2_ff0': mask_Bx1xSxS2_ff0, 'L0_xattn_ln1_s': _L0_xattn_in['ln1_s'], 'L0_xattn_ln1_b': _L0_xattn_in['ln1_b'], 'L0_xattn_w_qkv': _L0_xattn_in['w_qkv'], 'L0_xattn_b_qkv': _L0_xattn_in['b_qkv'], 'L0_xattn_w_ao': _L0_xattn_in['w_ao'], 'L0_xattn_b_ao': _L0_xattn_in['b_ao'], 'L0_xattn_ln2_s': _L0_xattn_in['ln2_s'], 'L0_xattn_ln2_b': _L0_xattn_in['ln2_b'], 'L0_xattn_w_q': _L0_xattn_in['w_q'], 'L0_xattn_b_q': _L0_xattn_in['b_q'], 'L0_xattn_w_kv': _L0_xattn_in['w_kv'], 'L0_xattn_b_kv': _L0_xattn_in['b_kv'], 'L0_xattn_w_co': _L0_xattn_in['w_co'], 'L0_xattn_b_co': _L0_xattn_in['b_co'], 'L0_xattn_ln3_s': _L0_xattn_in['ln3_s'], 'L0_xattn_ln3_b': _L0_xattn_in['ln3_b'], 'L0_xattn_w1': _L0_xattn_in['w1'], 'L0_xattn_b1': _L0_xattn_in['b1'], 'L0_xattn_w2': _L0_xattn_in['w2'], 'L0_xattn_b2': _L0_xattn_in['b2'], 'L1_xattn_Wq': _L1_xattn_in['Wq'], 'L1_xattn_bq': _L1_xattn_in['bq'], 'L1_xattn_Wk': _L1_xattn_in['Wk'], 'L1_xattn_bk': _L1_xattn_in['bk'], 'L1_xattn_Wv': _L1_xattn_in['Wv'], 'L1_xattn_bv': _L1_xattn_in['bv'], 'L1_xattn_Wo': _L1_xattn_in['Wo'], 'L1_xattn_bo': _L1_xattn_in['bo'], 'L1_xattn_gamma': _L1_xattn_in['gamma'], 'L1_xattn_beta': _L1_xattn_in['beta']}

def reference(x, ctx_2048, mask_1x1xSxS2_fc1, mask_Bx1xSxS2_ff1, mask_Bx1xSxS2_ff0, L0_xattn_ln1_s, L0_xattn_ln1_b, L0_xattn_w_qkv, L0_xattn_b_qkv, L0_xattn_w_ao, L0_xattn_b_ao, L0_xattn_ln2_s, L0_xattn_ln2_b, L0_xattn_w_q, L0_xattn_b_q, L0_xattn_w_kv, L0_xattn_b_kv, L0_xattn_w_co, L0_xattn_b_co, L0_xattn_ln3_s, L0_xattn_ln3_b, L0_xattn_w1, L0_xattn_b1, L0_xattn_w2, L0_xattn_b2, L1_xattn_Wq, L1_xattn_bq, L1_xattn_Wk, L1_xattn_bk, L1_xattn_Wv, L1_xattn_bv, L1_xattn_Wo, L1_xattn_bo, L1_xattn_gamma, L1_xattn_beta):
    import jax
    import jax.numpy as jnp

    def _L0_xattn_ref(hidden_states, encoder_states, ltor_mask, cross_mask, ln1_s, ln1_b, w_qkv, b_qkv, w_ao, b_ao, ln2_s, ln2_b, w_q, b_q, w_kv, b_kv, w_co, b_co, ln3_s, ln3_b, w1, b1, w2, b2):
        import jax, jax.numpy as jnp
        import numpy as np
        H = 256
        NH = 16
        HD = H // NH
        EPS = 1e-05

        def gelu(x):
            return 0.5 * x * (1.0 + jnp.tanh(0.7978845608028654 * x * (1.0 + 0.044715 * x * x)))

        def layernorm(x, scale, bias):
            m = jnp.mean(x, axis=-1, keepdims=True)
            v = jnp.mean(jnp.square(x - m), axis=-1, keepdims=True)
            return (x - m) * jax.lax.rsqrt(v + EPS) * scale + bias

        def split_heads(x):
            b, s, _ = x.shape
            return x.reshape(b, s, NH, HD).transpose(0, 2, 1, 3)

        def merge_heads(x):
            b, nh, s, hd = x.shape
            return x.transpose(0, 2, 1, 3).reshape(b, s, nh * hd)

        def attention(q, k, v, mask):
            scores = jnp.einsum('bhqd,bhkd->bhqk', q, k) / jnp.sqrt(jnp.float32(HD))
            scores = scores * mask - 10000.0 * (1.0 - mask)
            probs = jax.nn.softmax(scores, axis=-1)
            return jnp.einsum('bhqk,bhkd->bhqd', probs, v)
        ln_out = layernorm(hidden_states, ln1_s, ln1_b)
        qkv = ln_out @ w_qkv + b_qkv
        q, k, v = jnp.split(qkv, 3, axis=-1)
        ctx = merge_heads(attention(split_heads(q), split_heads(k), split_heads(v), ltor_mask))
        attn_out = ctx @ w_ao + b_ao
        x = hidden_states + attn_out
        ln_out = layernorm(x, ln2_s, ln2_b)
        q = ln_out @ w_q + b_q
        kv = encoder_states @ w_kv + b_kv
        k, v = jnp.split(kv, 2, axis=-1)
        ctx = merge_heads(attention(split_heads(q), split_heads(k), split_heads(v), cross_mask))
        cross_out = ctx @ w_co + b_co
        x = x + cross_out
        ln_out = layernorm(x, ln3_s, ln3_b)
        mlp_out = gelu(ln_out @ w1 + b1) @ w2 + b2
        return x + mlp_out

    def _L1_xattn_ref(hidden_state, encoder_hidden_state, encoder_attention_mask, Wq, bq, Wk, bk, Wv, bv, Wo, bo, gamma, beta):
        import jax, jax.numpy as jnp
        import numpy as np
        H = 256
        NH = 32
        KVH = 8
        HD = H // NH
        GROUPS = NH // KVH
        EPS = 1e-06
        B, L, S = (4, 128, 128)

        def _gqa_forward(hidden_state, encoder_hidden_state, encoder_attention_mask, Wq, bq, Wk, bk, Wv, bv, Wo, bo, gamma, beta):
            b, l, _ = hidden_state.shape
            s = encoder_hidden_state.shape[1]
            q = hidden_state @ Wq + bq
            k = encoder_hidden_state @ Wk + bk
            v = encoder_hidden_state @ Wv + bv
            q = q.reshape(b, l, KVH, GROUPS, HD).transpose(0, 2, 3, 1, 4)
            k = k.reshape(b, s, KVH, HD).transpose(0, 2, 1, 3)
            v = v.reshape(b, s, KVH, HD).transpose(0, 2, 1, 3)
            scale = 1.0 / jnp.sqrt(jnp.asarray(HD, q.dtype))
            scores = jnp.einsum('bkgld,bksd->bkgls', q, k) * scale
            scores = scores + encoder_attention_mask[:, :, None, :, :]
            attn = jax.nn.softmax(scores, axis=-1)
            out = jnp.einsum('bkgls,bksd->bkgld', attn, v)
            out = out.transpose(0, 3, 1, 2, 4).reshape(b, l, H)
            out = out @ Wo + bo
            x = out + hidden_state
            mu = jnp.mean(x, axis=-1, keepdims=True)
            var = jnp.var(x, axis=-1, keepdims=True)
            return (x - mu) * jax.lax.rsqrt(var + EPS) * gamma + beta
        return _gqa_forward(hidden_state, encoder_hidden_state, encoder_attention_mask, Wq, bq, Wk, bk, Wv, bv, Wo, bo, gamma, beta)
    x = _L0_xattn_ref(x, ctx_2048, mask_1x1xSxS2_fc1, mask_Bx1xSxS2_ff1, L0_xattn_ln1_s, L0_xattn_ln1_b, L0_xattn_w_qkv, L0_xattn_b_qkv, L0_xattn_w_ao, L0_xattn_b_ao, L0_xattn_ln2_s, L0_xattn_ln2_b, L0_xattn_w_q, L0_xattn_b_q, L0_xattn_w_kv, L0_xattn_b_kv, L0_xattn_w_co, L0_xattn_b_co, L0_xattn_ln3_s, L0_xattn_ln3_b, L0_xattn_w1, L0_xattn_b1, L0_xattn_w2, L0_xattn_b2)
    x = _L1_xattn_ref(x, ctx_2048, mask_Bx1xSxS2_ff0, L1_xattn_Wq, L1_xattn_bq, L1_xattn_Wk, L1_xattn_bk, L1_xattn_Wv, L1_xattn_bv, L1_xattn_Wo, L1_xattn_bo, L1_xattn_gamma, L1_xattn_beta)
    return x

_drawn_inputs = setup_inputs


def setup_inputs(seed=0):
    import zlib

    import numpy as np

    out = dict(_drawn_inputs(seed))
    spreads = {'L0_xattn_ln1_s': (1.0, 0.6),
     'L0_xattn_ln1_b': (0.0, 0.757),
     'L0_xattn_b_qkv': (0.0, 0.27),
     'L0_xattn_b_ao': (0.0, 0.1),
     'L0_xattn_ln2_s': (1.0, 0.6),
     'L0_xattn_ln2_b': (0.0, 2.0),
     'L0_xattn_b_q': (0.0, 2.0),
     'L0_xattn_b_kv': (0.0, 0.283),
     'L0_xattn_b_co': (0.0, 0.1),
     'L0_xattn_ln3_s': (1.0, 0.6),
     'L0_xattn_ln3_b': (0.0, 0.653),
     'L0_xattn_b1': (0.0, 0.27),
     'L0_xattn_b2': (0.0, 0.1),
     'L1_xattn_bq': (0.0, 0.8),
     'L1_xattn_bk': (0.0, 2.0),
     'L1_xattn_bv': (0.0, 0.281),
     'L1_xattn_bo': (0.0, 0.1),
     'L1_xattn_gamma': (1.0, 0.2),
     'L1_xattn_beta': (0.0, 0.1)}
    factors = {'L0_xattn_w_qkv': 3.144, 'L0_xattn_w_q': 8.0, 'L1_xattn_Wq': 8.0, 'L1_xattn_Wk': 8.0}
    for name, (base, spread) in spreads.items():
        noise = np.random.default_rng([zlib.crc32(name.encode()), seed]).standard_normal(out[name].shape)
        drawn = base * np.exp(spread * noise) if base else spread * noise
        out[name] = jnp.asarray(drawn.astype(out[name].dtype))
    for name, factor in factors.items():
        out[name] = (out[name] * factor).astype(out[name].dtype)
    return out
```

```python
from contextlib import ExitStack

import concourse.bass as bass
from concourse import mybir

F32 = mybir.dt.float32
ALU = mybir.AluOpType
ACT = mybir.ActivationFunctionType
AX = mybir.AxisListType

P = 128
SEQ = 64
D = 256
KC = D // P
SUB = 2
TOK = SUB * P
BPS = P // SEQ
NB = SUB * BPS
NSTREAM = 2
GROUPS = 8
HID = 1024
HC = HID // P
RING = 4

HEADS = {"S": 16, "C": 16, "G": 32}
JOINT = {a: HEADS[a] // GROUPS for a in "SCG"}
HD = {a: D // HEADS[a] for a in "SCG"}
PAIRW = {a: 2 * (HD[a] + 1) for a in "SCG"}
PAIRS = {a: HEADS[a] // 2 for a in "SCG"}
PT_JOBS = {a: PAIRS[a] // 4 for a in "SCG"}
VJOBS = {"S": 2, "C": 2, "G": 1}
EPS = {1: 1e-5, 2: 1e-5, 3: 1e-5, 4: 1e-6}


def schedule():
    steps = []

    def attention(a, after):
        return [
            ("QK", 0, a), ("SC", 0, a, 0), ("V", 0, a), ("SM", 0, a, 0),
            ("QK", 1, a), ("SC", 0, a, 1), ("V", 1, a), ("SM", 0, a, 1),
            ("SC", 1, a, 0), ("PV", 0, a, 0), ("SM", 1, a, 0),
            ("SC", 1, a, 1), ("PV", 0, a, 1), ("SM", 1, a, 1),
            ("CT", 0, a), ("PV", 1, a, 0), ("OP", 0, a), *after(0),
            ("PV", 1, a, 1), ("CT", 1, a), ("OP", 1, a), *after(1),
        ]

    for s in range(NSTREAM):
        steps += [("ET", s), ("XB", s, "S"), ("LN", s, 1)]
    steps += attention("S", lambda s: [("XB", s, "C"), ("LN", s, 2)])
    steps += attention("C", lambda s: [("XB", s, "M"), ("LN", s, 3)])
    for m in range(HC // 2):
        for s in range(NSTREAM):
            steps += [("H", s, m)]
        if m >= 1:
            for s in range(NSTREAM):
                steps += [("GE", s, m - 1)]
    for s in range(NSTREAM):
        steps += [("GE", s, HC // 2 - 1)]
    for s in range(NSTREAM):
        steps += [("Y", s), ("XB", s, "G"), ("XT", s)]
    steps += attention("G", lambda s: [("FN", s)])
    return steps


SCHEDULE = schedule()
DVE_LINKS = sum({"LN": 1, "FN": 1, "SM": 1, "PV": 1, "H": 1}.get(step[0], 0) for step in SCHEDULE)
POOL_LINKS = sum({"LN": 1, "FN": 2}.get(step[0], 0) for step in SCHEDULE)


def jobs_of(step):
    kind = step[0]
    if kind in ("ET", "LN", "XT", "CT"):
        return [("turn", "act")]
    if kind == "QK":
        return [("q", "act"), ("k", "dve")]
    if kind == "V":
        return [(f"v{n}", "dve") for n in range(VJOBS[step[2]])]
    if kind == "PV":
        return [(f"p{n}", "act") for n in range(PT_JOBS[step[2]])] + [("o", "dve")]
    if kind == "H":
        return [("h", "act")]
    if kind in ("OP", "Y"):
        return [("out", "dve")]
    return []


JOBS = [(step, job, taker) for step in SCHEDULE for job, taker in jobs_of(step)]


def steps_of(*kinds):
    return [step for step in SCHEDULE if step[0] in kinds]


class Signal:

    def __init__(self, sem, events, unit=1):
        self.sem, self.events, self.unit = sem, list(events), unit
        self.turn = len(self.events) * unit

    def now(self, event, it):
        return it * self.turn + (self.turn + (self.events.index(event) + 1) * self.unit)

    def before(self, event, it):
        return it * self.turn + (self.events.index(event) + 1) * self.unit


def build(nc, io, out, dve_chain, pool_chain):
    turns = io["x"].shape[0] * SEQ // (NSTREAM * TOK)

    with ExitStack() as ctx:
        def sb(name, *free):
            return ctx.enter_context(nc.sbuf_tensor(name, [P, *free], F32))

        def psum(name, *free):
            return ctx.enter_context(nc.psum_tensor(name, [P, *free], F32))

        def sem(name):
            return ctx.enter_context(nc.semaphore(name))

        w_qkv = sb("w_qkv", KC, 3 * D)
        w_ao = sb("w_ao", KC, D)
        w_q = sb("w_q", KC, D)
        w_kv = sb("w_kv", KC, 2 * D)
        w_co = sb("w_co", KC, D)
        w_1 = sb("w_1", KC, HID)
        w_2 = sb("w_2", HC, D)
        g_q = sb("g_q", KC, D)
        g_kn = sb("g_kn", KC, 64)
        g_k = sb("g_k", KC, D)
        g_v = sb("g_v", KC, 64)
        g_o = sb("g_o", KC, D)
        w_of = {"S": (w_qkv[:, :, 0:D], w_qkv[:, :, D:2 * D], w_qkv[:, :, 2 * D:3 * D], w_ao),
                "C": (w_q, w_kv[:, :, 0:D], w_kv[:, :, D:2 * D], w_co),
                "G": (g_q, g_k, g_v, g_o)}
        col_ln = {n: (sb(f"ln{n}_s", KC), sb(f"ln{n}_b", KC)) for n in (1, 2, 3)}
        col_q = {a: sb(f"bias_q_{a}", KC) for a in "SCG"}
        col_k = {a: sb(f"bias_k_{a}", KC) for a in "SCG"}
        col_1 = sb("bias_1", HC)
        row_k = sb("row_k", 8, 4, 8)
        row_kn = sb("row_kn", 64)
        row_v = {a: sb(f"bias_v_{a}", 64 if a == "G" else D) for a in "SCG"}
        row_o = {a: sb(f"bias_o_{a}", D) for a in "SCMG"}
        gamma = sb("gamma", D)
        beta = sb("beta", D)
        ident = sb("ident", P)
        ones1 = sb("ones1", 1)
        neghalf = sb("neghalf", SUB)
        onehot = {2: sb("onehot2", 4, 2), 4: sb("onehot4", 4, 4)}
        headmask = {2: sb("headmask2", 2), 4: sb("headmask4", 4)}
        mask_s = sb("mask_s", SEQ)
        off_s = sb("off_s", SEQ)

        xin = sb("xin", NSTREAM, SUB, D)
        ein = sb("ein", NSTREAM, SUB, D)
        mask_c = sb("mask_c", NSTREAM, SUB, SEQ)
        off_c = sb("off_c", NSTREAM, SUB, SEQ)
        mask_g = sb("mask_g", NSTREAM, SUB, SEQ)

        both = range(NSTREAM)
        xr = [sb(f"xr{s}", SUB, D) for s in both]
        xb = [sb(f"xb{s}", SUB, D) for s in both]
        z = [sb(f"z{s}", SUB, D) for s in both]
        stats = [sb(f"stats{s}", SUB, 6) for s in both]
        mv = [sb(f"mv{s}", SUB, 2) for s in both]
        veps = [sb(f"veps{s}", SUB) for s in both]
        rstd = [sb(f"rstd{s}", SUB) for s in both]
        zT = [sb(f"zT{s}", KC, TOK) for s in both]
        eT = [sb(f"eT{s}", KC, TOK) for s in both]
        qT = [sb(f"qT{s}", KC, TOK) for s in both]
        kbd = [sb(f"kbd{s}", KC, 4, TOK) for s in both]
        vb = {"L": [sb(f"vb{s}", NB, GROUPS, PAIRW["S"]) for s in both],
              "G": [sb(f"vg{s}", NB, GROUPS, PAIRW["G"]) for s in both]}
        attn_rows = [sb(f"attn{s}", SUB, D) for s in both]
        cT = [sb(f"cT{s}", KC, TOK) for s in both]
        res = [sb(f"res{s}", SUB, D) for s in both]
        su = [[sb(f"su{s}{t}", 2048) for t in range(SUB)] for s in both]
        pT = [sb(f"pT{t}", 2048) for t in range(SUB)]
        mx = [sb(f"mx{s}", 32) for s in both]
        rden = [sb(f"rden{s}", 32) for s in both]

        scores = psum("scores", 4, 512)
        ring = [psum(f"ring{n}", 512) for n in range(RING)]

        s_w1st = sem("weights_self_loaded")
        s_wrest = sem("weights_rest_loaded")
        s_small = sem("small_loaded")
        s_const = sem("constants_made")
        s_kbias = sem("gqa_key_bias_turned")
        s_prep = sem("operands_prepared")
        s_pre = sem("prologue_chain")
        s_prepool = sem("prologue_pool_chain")
        s_dve = sem("dve_chain")
        s_pool = sem("pool_chain")
        s_stand = sem("waits_met")
        one = ["turn"]
        x_loaded = Signal(sem("x_loaded"), one, 16)
        e_loaded = Signal(sem("e_loaded"), one, 16)
        mc_loaded = Signal(sem("mask_c_loaded"), one, 16)
        mg_loaded = Signal(sem("mask_g_loaded"), one, 16)
        stored = [Signal(sem(f"stored{s}"), one, 16) for s in both]
        filled = Signal(sem("bank_filled"), [(st, j) for st, j, _ in JOBS])
        by_act = Signal(sem("bank_emptied_by_act"), [(st, j) for st, j, e in JOBS if e == "act"])
        by_dve = Signal(sem("bank_emptied_by_dve"), [(st, j) for st, j, e in JOBS if e == "dve"])
        scored = Signal(sem("scores_filled"), steps_of("SC"))
        masked = Signal(sem("scores_masked"), steps_of("SC"))
        offset = Signal(sem("mask_offset_added"), [st for st in steps_of("SC") if st[2] != "G"])
        shifted = Signal(sem("row_max_subtracted"), steps_of("SM"))
        probs = Signal(sem("probs_ready"), steps_of("SM"))
        moments = Signal(sem("moments_ready"), steps_of("LN", "FN"))
        scaled = Signal(sem("rstd_ready"), steps_of("LN", "FN"))
        normed = Signal(sem("normed_ready"), steps_of("LN", "FN"))
        biased = Signal(sem("residual_biased"), steps_of("XB"))
        offmask = Signal(sem("cross_offset_ready"), one)
        cubic = Signal(sem("gelu_argument_ready"), steps_of("H"))
        tanhed = Signal(sem("gelu_tanh_ready"), steps_of("GE"))
        gelued = Signal(sem("gelu_ready"), steps_of("GE"))
        finished = Signal(sem("result_ready"), steps_of("FN"))

        def credit(eng, *signals):
            for s in signals:
                eng.sem_inc(s.sem, s.turn)

        def wait(eng, signal, event, it):
            eng.wait_ge(signal.sem, signal.now(event, it))

        def wait_before(eng, signal, event, it):
            eng.wait_ge(signal.sem, signal.before(event, it))

        def stand(eng):
            eng.sem_inc(s_stand, 1)

        def cross(a):
            return "G" if a == "G" else "L"

        def score_view(a):
            return scores[:, :, 0:KC * JOINT[a] * SEQ].rearrange("p i (h k) -> p i h k", k=SEQ)

        def su_view(s, a, t):
            return su[s][t][:, 0:HEADS[a] * SEQ]

        def rows(dram):
            return dram.rearrange("(k p) n -> p k n", p=P)

        def row_of(vec):
            return vec.rearrange("(a n) -> a n", a=1)

        def column_of(vec):
            return vec.rearrange("(c p) -> p c", p=P)

        index = {(st, j): n for n, (st, j, _) in enumerate(JOBS)}

        def bank(step, job):
            return index[(step, job)] % RING

        block = ctx.enter_context(nc.Block())

        @block.sync
        def _(sp):
            n_it = NSTREAM * SUB
            x_v = io["x"].flatten_outer_dims().rearrange("(n t p) d -> n p t d", t=n_it, p=P)
            e_v = io["ctx"].flatten_outer_dims().rearrange("(n t p) d -> n p t d", t=n_it, p=P)
            mc_v = io["mask_c"].flatten_outer_dims().rearrange("(n t p) k -> n p t k", t=n_it, p=P)
            mg_v = io["mask_g"].flatten_outer_dims().rearrange("(n t p) k -> n p t k", t=n_it, p=P)
            o_v = out.flatten_outer_dims().rearrange("(n t p) d -> n p t d", t=SUB, p=P)

            def load(tile, dram, signal, it):
                sp.dma_start(tile[:].rearrange("p s t d -> p (s t) d"), dram[it]).then_inc(signal.sem, 16)

            load(ein, e_v, e_loaded, 0)
            load(xin, x_v, x_loaded, 0)
            for tile, name in ((w_qkv, "w_qkv"), (w_ao, "w_ao")):
                sp.dma_start(tile[:], rows(io[name])).then_inc(s_w1st, 16)
            load(mask_c, mc_v, mc_loaded, 0)
            load(mask_g, mg_v, mg_loaded, 0)
            for tile, name in ((w_q, "w_q"), (w_kv, "w_kv"), (w_co, "w_co"), (w_1, "w_1"), (w_2, "w_2"),
                               (g_q, "Wq"), (g_kn, "Wk"), (g_v, "Wv"), (g_o, "Wo")):
                sp.dma_start(tile[:], rows(io[name])).then_inc(s_wrest, 16)
            credit(sp, *stored, x_loaded, e_loaded, mc_loaded, mg_loaded)
            with sp.Fori(1, turns) as it:
                wait_before(sp, filled, (("ET", 1), "turn"), it)
                stand(sp)
                load(ein, e_v, e_loaded, it)
                wait_before(sp, normed, ("LN", 1, 1), it)
                stand(sp)
                wait_before(sp, biased, ("XB", 1, "S"), it)
                stand(sp)
                load(xin, x_v, x_loaded, it)
                wait_before(sp, masked, ("SC", 1, "C", 1), it)
                stand(sp)
                wait_before(sp, offmask, "turn", it)
                stand(sp)
                load(mask_c, mc_v, mc_loaded, it)
                wait_before(sp, masked, ("SC", 1, "G", 1), it)
                stand(sp)
                load(mask_g, mg_v, mg_loaded, it)
                for s in both:
                    wait_before(sp, finished, ("FN", s), it)
                    stand(sp)
                    sp.dma_start(o_v[it * NSTREAM + (s - NSTREAM)], res[s][:]).then_inc(stored[s].sem, 16)
            for s in both:
                sp.wait_ge(finished.sem, finished.now(("FN", s), turns - 1))
                sp.dma_start(o_v[(turns - 1) * NSTREAM + s], res[s][:]).then_inc(stored[s].sem, 16)
            for s in both:
                sp.wait_ge(stored[s].sem, (turns + 1) * stored[s].turn)

        small = 0

        @block.scalar
        def _(act):
            nonlocal small
            for n in (1, 2, 3):
                for tile, name in zip(col_ln[n], (f"ln{n}_s", f"ln{n}_b")):
                    act.dma_start(tile[:], column_of(io[name]), allow_slow_non_contiguous=True).then_inc(s_small, 16)
                    small += 16
            cols = ((col_q["S"], io["b_qkv"][0:D]), (col_k["S"], io["b_qkv"][D:2 * D]), (col_q["C"], io["b_q"]),
                    (col_k["C"], io["b_kv"][0:D]), (col_q["G"], io["bq"]), (col_1, io["b1"]))
            for tile, src in cols:
                act.dma_start(tile[:], column_of(src), allow_slow_non_contiguous=True).then_inc(s_small, 16)
                small += 16
            spread = ((row_v["S"], io["b_qkv"][2 * D:3 * D]), (row_v["C"], io["b_kv"][D:2 * D]), (row_v["G"], io["bv"]),
                      (row_o["S"], io["b_ao"]), (row_o["C"], io["b_co"]), (row_o["M"], io["b2"]),
                      (row_o["G"], io["bo"]), (gamma, io["gamma"]), (beta, io["beta"]))
            for tile, src in spread:
                act.dma_start(tile[:], row_of(src).broadcast_to([P, src.shape[0]])).then_inc(s_small, 16)
                small += 16
            act.dma_start(row_kn[0:1, :], row_of(io["bk"])).then_inc(s_small, 16)
            small += 16
            for h in range(BPS):
                act.dma_start(mask_s[h * SEQ:(h + 1) * SEQ, :], io["mask_s"][0, 0]).then_inc(s_small, 16)
                small += 16
            credit(act, by_act, probs, tanhed)
            act.wait_ge(s_small, small)
            act.wait_ge(s_prep, 1)

            def empty_turned(step, dst, it, n=None):
                wait(act, filled, (step, "turn"), it)
                src = ring[bank(step, "turn")][:].rearrange("p (k n) -> p k n", k=KC)
                if n is None:
                    nc.scalar.copy(dst[:], src).then_inc(by_act.sem, 1)
                    return
                for k in range(KC):
                    last = nc.scalar.activation(dst[:, k, :], src[:, k, :], ACT.Identity,
                                                bias=col_ln[n][1][:, k:k + 1], scale=col_ln[n][0][:, k:k + 1])
                last.then_inc(by_act.sem, 1)

            with act.Fori(0, turns) as it:
                for step in SCHEDULE:
                    kind, s = step[0], step[1]
                    if kind == "ET":
                        empty_turned(step, eT[s], it)
                    elif kind == "LN":
                        empty_turned(step, zT[s], it, step[2])
                    elif kind == "XT":
                        empty_turned(step, zT[s], it)
                    elif kind == "CT":
                        empty_turned(step, cT[s], it)
                    elif kind == "QK":
                        a = step[2]
                        wait(act, filled, (step, "q"), it)
                        src = ring[bank(step, "q")][:].rearrange("p (k n) -> p k n", k=KC)
                        for k in range(KC):
                            last = nc.scalar.activation(qT[s][:, k, :], src[:, k, :], ACT.Identity,
                                                        bias=col_q[a][:, k:k + 1], scale=HD[a] ** -0.5)
                        last.then_inc(by_act.sem, 1)
                    elif kind == "SM":
                        a, t = step[2:]
                        wait(act, shifted, step, it)
                        nc.scalar.activation(su_view(s, a, t), su_view(s, a, t), ACT.Exp).then_inc(probs.sem, 1)
                    elif kind == "PV":
                        a, t = step[2:]
                        for n in range(PT_JOBS[a]):
                            wait(act, filled, (step, f"p{n}"), it)
                            nc.scalar.copy(pT[t][:, n * 512:(n + 1) * 512],
                                           ring[bank(step, f"p{n}")][:]).then_inc(by_act.sem, 1)
                    elif kind == "H":
                        m = step[2]
                        wait(act, filled, (step, "h"), it)
                        for k in range(2):
                            c, lo = 2 * m + k, (2 * m + k) * TOK
                            src = ring[bank(step, "h")][:, k * TOK:(k + 1) * TOK]
                            nc.scalar.activation(su[s][0][:, lo:lo + TOK], src, ACT.Identity, bias=col_1[:, c:c + 1])
                            last = nc.scalar.activation(su[s][1][:, lo:lo + TOK], src, ACT.Square,
                                                        bias=col_1[:, c:c + 1])
                        last.then_inc(by_act.sem, 1)
                    elif kind == "GE":
                        m = step[2]
                        part = su[s][1][:, m * 512:(m + 1) * 512]
                        wait(act, cubic, ("H", s, m), it)
                        nc.scalar.activation(part, part, ACT.Tanh, scale=0.7978845608028654).then_inc(tanhed.sem, 1)

        @block.gpsimd
        def _(pool):
            chain = [0]

            def pre(ins):
                chain[0] += 1
                ins.then_inc(s_prepool, 1)
                pool.wait_ge(s_prepool, chain[0])

            pre(pool.memset(ident[:], 0.0))
            pre(pool.affine_select(out=ident[:], in_=ident[:], compare_op=ALU.not_equal, fill=1.0, base=0,
                                   pattern=[[-1, P]], channel_multiplier=1))
            pre(pool.memset(ones1[:], 1.0))
            pre(pool.memset(neghalf[:], -0.5))
            for g in (2, 4):
                w = 32 // g
                m = onehot[g]
                pre(pool.memset(m[:], 1.0))
                pre(pool.affine_select(out=m[:], in_=m[:], compare_op=ALU.is_ge, fill=0.0, base=0,
                                       pattern=[[-32, 4], [-w, g]], channel_multiplier=1))
                pre(pool.affine_select(out=m[:], in_=m[:], compare_op=ALU.is_ge, fill=0.0, base=w - 1,
                                       pattern=[[32, 4], [w, g]], channel_multiplier=-1))
            pool.sem_inc(s_const, 1)
            credit(pool, offset, scaled, biased, offmask, finished)
            pool.wait_ge(s_prep, 1)

            with pool.Fori(0, turns) as it:
                links = [0]

                def link(ins):
                    links[0] += 1
                    ins.then_inc(s_pool, 1)
                    pool.wait_ge(s_pool, it * pool_chain + links[0])

                for step in SCHEDULE:
                    kind, s = step[0], step[1]
                    if kind == "XB":
                        a = step[2]
                        bias = row_o[a][:, :].unsqueeze(1).to_broadcast([P, SUB, D])
                        if a == "S":
                            wait(pool, x_loaded, "turn", it)
                            wait_before(pool, by_dve, (("OP", s, "G"), "out"), it)
                        else:
                            made = {"C": ("OP", s, "S"), "M": ("OP", s, "C"), "G": ("Y", s)}[a]
                            wait(pool, by_dve, (made, "out"), it)
                        pool.tensor_tensor(xb[s][:], (xin[:, s] if a == "S" else xr[s][:]), bias,
                                           ALU.add).then_inc(biased.sem, 1)
                        if step == ("XB", 0, "S"):
                            wait(pool, mc_loaded, "turn", it)
                            stand(pool)
                            pool.tensor_scalar(off_c[:], mask_c[:], -1.0, 10000.0, ALU.add,
                                               ALU.mult).then_inc(offmask.sem, 1)
                    elif kind in ("LN", "FN"):
                        wait(pool, moments, step, it)
                        stand(pool)
                        link(pool.tensor_scalar(veps[s][:], mv[s][:, :, 1], EPS[4 if kind == "FN" else step[2]], 1.0,
                                                ALU.add, ALU.mult))
                        pool.tensor_tensor(rstd[s][:], veps[s][:], neghalf[:], ALU.pow).then_inc(scaled.sem, 1)
                        if kind == "FN":
                            wait(pool, normed, step, it)
                            link(pool.tensor_tensor(res[s][:], res[s][:],
                                                    gamma[:, :].unsqueeze(1).to_broadcast([P, SUB, D]), ALU.mult))
                            pool.tensor_tensor(res[s][:], res[s][:],
                                               beta[:, :].unsqueeze(1).to_broadcast([P, SUB, D]),
                                               ALU.add).then_inc(finished.sem, 1)
                    elif kind == "SC" and step[2] != "G":
                        a, t = step[2:]
                        off = off_s[:, :] if a == "S" else off_c[:, s, t]
                        if step == ("SC", 0, "C", 0):
                            wait(pool, offmask, "turn", it)
                        wait(pool, masked, step, it)
                        v = su_view(s, a, t).rearrange("p (h k) -> p h k", k=SEQ)
                        pool.tensor_tensor(v, v, off.unsqueeze(1).to_broadcast([P, HEADS[a], SEQ]),
                                           ALU.add).then_inc(offset.sem, 1)
                assert links[0] == pool_chain, links[0]

        @block.vector
        def _(dve):
            chain = [0]

            def pre(ins):
                chain[0] += 1
                ins.then_inc(s_pre, 1)
                dve.wait_ge(s_pre, chain[0])

            for s in both:
                for key, a in (("L", "S"), ("G", "G")):
                    v, w = vb[key][s], HD[a] + 1
                    pre(dve.memset(v[:], 0.0))
                    for j in range(2):
                        pre(dve.memset(v[64 * j:64 * j + 64, :, :, w * j + w - 1:w * j + w], 1.0))
            dve.wait_ge(s_small, small)
            pre(dve.tensor_scalar(off_s[:], mask_s[:], -1.0, 10000.0, ALU.add, ALU.mult))
            for a in "SCG":
                pre(dve.tensor_scalar(col_q[a][:], col_q[a][:], HD[a] ** -0.5, None, ALU.mult))
            pre(dve.tensor_copy(row_k[0:1], row_kn[0:1, :].rearrange("p (h d) -> p h d", d=8).unsqueeze(2)
                                .to_broadcast([1, 8, 4, 8])))
            dve.wait_ge(s_const, 1)
            dve.wait_ge(s_prepool, 10)
            for g in (2, 4):
                pre(dve.tensor_reduce(headmask[g][:], onehot[g][:].rearrange("p i j -> p j i"), AX.X, ALU.add))
            dve.sem_inc(s_prep, 1)
            dve.wait_ge(s_kbias, 1)
            pre(dve.tensor_copy(col_k["G"][:], ring[0][:, 0:KC]))
            dve.wait_ge(s_wrest, 16 * 9)
            for k in range(KC):
                pre(dve.tensor_copy(g_k[:, k, :].rearrange("p (h g d) -> p h g d", g=4, d=8),
                                    g_kn[:, k, :].rearrange("p (h d) -> p h d", d=8).unsqueeze(2)
                                    .to_broadcast([P, 8, 4, 8])))
            dve.sem_inc(s_prep, 1)
            credit(dve, by_dve, masked, shifted, moments, normed, cubic, gelued)

            with dve.Fori(0, turns) as it:
                links = [0]

                def link(ins):
                    links[0] += 1
                    ins.then_inc(s_dve, 1)
                    dve.wait_ge(s_dve, it * dve_chain + links[0])

                for step in SCHEDULE:
                    kind, s = step[0], step[1]
                    if kind in ("LN", "FN"):
                        if kind == "LN" and step[2] == 1:
                            wait(dve, x_loaded, "turn", it)
                            src, dst = xin[:, s], z[s]
                        else:
                            src, dst = xr[s][:], (res[s] if kind == "FN" else z[s])
                        for t in range(SUB):
                            last = dve.bn_stats(stats[s][:, t, :], src[:, t, :])
                        link(last)
                        stand(dve)
                        for t in range(SUB):
                            last = dve.bn_aggr(mv[s][:, t, :], stats[s][:, t, :])
                        last.then_inc(moments.sem, 1)
                        dve.wait_ge(moments.sem, moments.now(step, it))
                        wait(dve, scaled, step, it)
                        if kind == "FN":
                            wait_before(dve, stored[s], "turn", it)
                        for t in range(SUB):
                            last = dve.tensor_scalar(dst[:, t, :], src[:, t, :], mv[s][:, t, 0:1],
                                                     rstd[s][:, t:t + 1], ALU.subtract, ALU.mult)
                        last.then_inc(normed.sem, 1)
                    elif kind == "QK":
                        a = step[2]
                        g = JOINT[a]
                        wait(dve, filled, (step, "k"), it)
                        src = ring[bank(step, "k")][:].rearrange("p (k n) -> p k n", k=KC)
                        for k in range(KC):
                            for j in range(g):
                                last = dve.tensor_scalar(kbd[s][:, k, j, :], src[:, k, :], col_k[a][:, k:k + 1],
                                                         headmask[g][:, j:j + 1], ALU.add, ALU.mult)
                        last.then_inc(by_dve.sem, 1)
                    elif kind == "V":
                        a = step[2]
                        v, w = vb[cross(a)][s], HD[a] + 1
                        per = NB // VJOBS[a]
                        for n in range(VJOBS[a]):
                            wait(dve, filled, (step, f"v{n}"), it)
                            for j in range(2):
                                half = slice(64 * j, 64 * j + 64)
                                dst = v[half, n * per:(n + 1) * per, :, w * j:w * j + w - 1]
                                src = ring[bank(step, f"v{n}")][half, 0:per * (64 if a == "G" else D)]
                                if a == "G":
                                    src = src.rearrange("p (b h d) -> p b h d", b=per, d=HD[a])
                                    bias = row_v[a][half, :].rearrange("p (h d) -> p h d", d=HD[a])
                                else:
                                    src = src.rearrange("p (b h j d) -> p b h j d", b=per, j=2, d=HD[a])[:, :, :, j, :]
                                    bias = row_v[a][half, :].rearrange("p (h j d) -> p h j d", j=2, d=HD[a])[:, :, j, :]
                                last = dve.tensor_tensor(dst, src, bias.unsqueeze(1).to_broadcast(
                                    [64, per, GROUPS, HD[a]]), ALU.add)
                            last.then_inc(by_dve.sem, 1)
                    elif kind == "SC":
                        a, t = step[2:]
                        m = {"S": mask_s[:, :], "C": mask_c[:, s, t], "G": mask_g[:, s, t]}[a]
                        if step == ("SC", 0, "C", 0):
                            wait(dve, mc_loaded, "turn", it)
                        if step == ("SC", 0, "G", 0):
                            wait(dve, mg_loaded, "turn", it)
                        wait(dve, scored, step, it)
                        h = HEADS[a] // 4
                        dve.tensor_tensor(su_view(s, a, t).rearrange("p (i h k) -> p i h k", i=4, k=SEQ), score_view(a),
                                          m.unsqueeze(1).unsqueeze(1).to_broadcast([P, 4, h, SEQ]),
                                          ALU.add if a == "G" else ALU.mult).then_inc(masked.sem, 1)
                    elif kind == "SM":
                        a, t = step[2:]
                        if a == "G":
                            dve.wait_ge(masked.sem, masked.now(("SC", *step[1:]), it))
                        else:
                            wait(dve, offset, ("SC", *step[1:]), it)
                        v = su_view(s, a, t).rearrange("p (h k) -> p h k", k=SEQ)
                        top = mx[s][:, 0:HEADS[a]]
                        link(dve.tensor_reduce(top, v, AX.X, ALU.max))
                        dve.tensor_tensor(v, v, top.unsqueeze(2).to_broadcast([P, HEADS[a], SEQ]),
                                          ALU.subtract).then_inc(shifted.sem, 1)
                    elif kind == "PV":
                        a, t = step[2:]
                        n, w = HEADS[a], HD[a] + 1
                        wait(dve, filled, (step, "o"), it)
                        o = ring[bank(step, "o")][:, 0:n * w].rearrange("p (h d) -> p h d", d=w)
                        link(dve.reciprocal(rden[s][:, 0:n], o[:, :, w - 1]))
                        dve.tensor_tensor(attn_rows[s][:, t, :].rearrange("p (h d) -> p h d", d=w - 1), o[:, :, 0:w - 1],
                                          rden[s][:, 0:n].unsqueeze(2).to_broadcast([P, n, w - 1]),
                                          ALU.mult).then_inc(by_dve.sem, 1)
                    elif kind == "OP":
                        wait(dve, biased, ("XB", *step[1:]), it)
                        wait(dve, filled, (step, "out"), it)
                        dve.tensor_tensor(xr[s][:].rearrange("p t d -> p (t d)"), ring[bank(step, "out")][:],
                                          xb[s][:].rearrange("p t d -> p (t d)"), ALU.add).then_inc(by_dve.sem, 1)
                        dve.wait_ge(by_dve.sem, by_dve.now((step, "out"), it))
                    elif kind == "Y":
                        wait(dve, biased, ("XB", s, "M"), it)
                        wait(dve, filled, (step, "out"), it)
                        dve.scalar_tensor_tensor(out=xr[s][:].rearrange("p t d -> p (t d)"),
                                                 in0=ring[bank(step, "out")][:], scalar=0.5,
                                                 in1=xb[s][:].rearrange("p t d -> p (t d)"), op0=ALU.mult,
                                                 op1=ALU.add).then_inc(by_dve.sem, 1)
                    elif kind == "H":
                        m = step[2]
                        hid, sq = su[s][0][:, m * 512:(m + 1) * 512], su[s][1][:, m * 512:(m + 1) * 512]
                        wait(dve, by_act, (step, "h"), it)
                        link(dve.tensor_scalar(sq, sq, 0.044715, 1.0, ALU.mult, ALU.add))
                        dve.tensor_tensor(sq, sq, hid, ALU.mult).then_inc(cubic.sem, 1)
                    elif kind == "GE":
                        m = step[2]
                        hid, th = su[s][0][:, m * 512:(m + 1) * 512], su[s][1][:, m * 512:(m + 1) * 512]
                        wait(dve, tanhed, step, it)
                        dve.scalar_tensor_tensor(out=hid, in0=th, scalar=1.0, in1=hid, op0=ALU.add,
                                                 op1=ALU.mult).then_inc(gelued.sem, 1)
                assert links[0] == dve_chain, links[0]

        @block.tensor
        def _(pe):
            pe.wait_ge(s_prep, 1)
            for k in range(KC):
                last = nc.tensor.matmul(ring[0][:, k:k + 1], row_k[0:1].rearrange("p h g d -> p (h g d)")[:, k * P:(k + 1) * P],
                                        ones1[0:1, :], start=True, stop=True)
            last.then_inc(s_kbias, 1)
            pe.wait_ge(s_w1st, 32)
            pe.wait_ge(s_prep, 2)
            credit(pe, filled, scored)

            def claim(step, job, it):
                n = index[(step, job)]
                last = [m for m in range(n) if m % RING == n % RING]
                st, j, taker = JOBS[last[-1]] if last else JOBS[max(m for m in range(len(JOBS)) if m % RING == n % RING)]
                signal = by_act if taker == "act" else by_dve
                (wait if last else wait_before)(pe, signal, (st, j), it)
                return ring[n % RING]

            def turn_rows(step, src, it):
                b = claim(step, "turn", it)
                for k in range(KC):
                    for t in range(SUB):
                        last = nc.tensor.transpose(b[:, k * TOK + t * P:k * TOK + (t + 1) * P],
                                                   src[:, t, k * P:(k + 1) * P], ident[:])
                last.then_inc(filled.sem, 1)

            def project_cols(step, job, w, src, it, m0=0):
                b = claim(step, job, it)
                for m in range(2):
                    for k in range(KC):
                        last = nc.tensor.matmul(b[:, m * TOK:(m + 1) * TOK], w[:, k, (m0 + m) * P:(m0 + m + 1) * P],
                                                src[:, k, :], start=(k == 0), stop=(k == KC - 1))
                last.then_inc(filled.sem, 1)

            with pe.Fori(0, turns) as it:
                for step in SCHEDULE:
                    kind, s = step[0], step[1]
                    if kind == "ET":
                        if s == 0:
                            wait(pe, e_loaded, "turn", it)
                        turn_rows(step, ein[:, s], it)
                    elif kind == "LN":
                        wait(pe, normed, step, it)
                        turn_rows(step, z[s], it)
                    elif kind == "XT":
                        wait(pe, by_dve, (("Y", s), "out"), it)
                        turn_rows(step, xr[s], it)
                    elif kind == "CT":
                        wait(pe, by_dve, (("PV", s, step[2], SUB - 1), "o"), it)
                        turn_rows(step, attn_rows[s], it)
                    elif kind == "QK":
                        a = step[2]
                        made = {"S": ("LN", s, 1), "C": ("LN", s, 2), "G": ("XT", s)}[a]
                        wait(pe, by_act, (made, "turn"), it)
                        project_cols(step, "q", w_of[a][0], zT[s], it)
                        project_cols(step, "k", w_of[a][1], zT[s] if a == "S" else eT[s], it)
                    elif kind == "V":
                        a = step[2]
                        src, w, width = (zT[s] if a == "S" else eT[s]), w_of[a][2], (64 if a == "G" else D)
                        per = NB // VJOBS[a]
                        for n in range(VJOBS[a]):
                            b = claim(step, f"v{n}", it)
                            for q in range(per):
                                seq = n * per + q
                                for k in range(KC):
                                    for j in range(2):
                                        last = nc.tensor.matmul(b[64 * j:64 * j + 64, q * width:(q + 1) * width],
                                                                src[:, k, seq * SEQ:(seq + 1) * SEQ], w[:, k, :],
                                                                start=(k == 0), stop=(k == KC - 1))
                            last.then_inc(filled.sem, 1)
                    elif kind == "SC":
                        a, t = step[2:]
                        g = JOINT[a]
                        wait(pe, by_act, (("QK", s, a), "q"), it)
                        wait(pe, by_dve, (("QK", s, a), "k"), it)
                        at = scored.events.index(step)
                        if at:
                            wait(pe, masked, scored.events[at - 1], it)
                        else:
                            wait_before(pe, masked, scored.events[-1], it)
                        for k in range(KC):
                            for flip in range(2):
                                for i in range(4):
                                    b = (i + flip) % 2
                                    r, tok = slice(32 * i, 32 * i + 32), t * P + b * SEQ
                                    dst = scores[64 * b:64 * b + 64, i, k * g * SEQ:(k + 1) * g * SEQ]
                                    last = nc.tensor.matmul(dst.rearrange("p (j k) -> p j k", k=SEQ),
                                                            qT[s][r, k, tok:tok + SEQ], kbd[s][r, k, 0:g, tok:tok + SEQ],
                                                            start=True, stop=True)
                        last.then_inc(scored.sem, 1)
                    elif kind == "PV":
                        a, t = step[2:]
                        wait(pe, probs, ("SM", *step[1:]), it)
                        for n in range(PT_JOBS[a]):
                            b = claim(step, f"p{n}", it)
                            for c in range(4):
                                lo = (4 * n + c) * P
                                last = nc.tensor.transpose(b[:, c * P:(c + 1) * P], su[s][t][:, lo:lo + P], ident[:])
                            last.then_inc(filled.sem, 1)
                        b = claim(step, "o", it)
                        wait(pe, by_act, (step, f"p{PT_JOBS[a] - 1}"), it)
                        if t == 0:
                            wait(pe, by_dve, (("V", s, a), f"v{VJOBS[a] - 1}"), it)
                        g2, w = JOINT[a] // 2, PAIRW[a]
                        for pair in range(PAIRS[a]):
                            i, k, jj = pair // (KC * g2), pair // g2 % KC, pair % g2
                            group = 4 * k + i
                            at = (group * g2 + jj) * w
                            for q in range(BPS):
                                last = nc.tensor.matmul(b[64 * q:64 * q + 64, at:at + w],
                                                        pT[t][:, pair * P + q * SEQ:pair * P + (q + 1) * SEQ],
                                                        vb[cross(a)][s][:, t * BPS + q, group, :], start=True, stop=True)
                        last.then_inc(filled.sem, 1)
                    elif kind == "OP":
                        b = claim(step, "out", it)
                        wait(pe, by_act, (("CT", *step[1:]), "turn"), it)
                        for t in range(SUB):
                            for k in range(KC):
                                last = nc.tensor.matmul(b[:, t * D:(t + 1) * D], cT[s][:, k, t * P:(t + 1) * P],
                                                        w_of[step[2]][3][:, k, :], start=(k == 0), stop=(k == KC - 1))
                        last.then_inc(filled.sem, 1)
                    elif kind == "H":
                        wait(pe, by_act, (("LN", s, 3), "turn"), it)
                        project_cols(step, "h", w_1, zT[s], it, 2 * step[2])
                    elif kind == "Y":
                        b = claim(step, "out", it)
                        wait(pe, gelued, ("GE", s, HC // 2 - 1), it)
                        for t in range(SUB):
                            for m in range(HC):
                                lo = m * TOK + t * P
                                last = nc.tensor.matmul(b[:, t * D:(t + 1) * D], su[s][0][:, lo:lo + P], w_2[:, m, :],
                                                        start=(m == 0), stop=(m == HC - 1))
                        last.then_inc(filled.sem, 1)


NAMES = {"x": "x", "ctx": "ctx_2048", "mask_s": "mask_1x1xSxS2_fc1", "mask_c": "mask_Bx1xSxS2_ff1",
         "mask_g": "mask_Bx1xSxS2_ff0",
         **{n: f"L0_xattn_{n}" for n in ("ln1_s", "ln1_b", "w_qkv", "b_qkv", "w_ao", "b_ao", "ln2_s", "ln2_b", "w_q",
                                         "b_q", "w_kv", "b_kv", "w_co", "b_co", "ln3_s", "ln3_b", "b1", "b2")},
         "w_1": "L0_xattn_w1", "w_2": "L0_xattn_w2",
         **{n: f"L1_xattn_{n}" for n in ("Wq", "bq", "Wk", "bk", "Wv", "bv", "Wo", "bo", "gamma", "beta")}}


def kernel(**inputs):
    import numpy as np
    import concourse.bacc as bacc
    from concourse.bass_utils import run_bass_kernel_spmd as run

    nc = bacc.Bacc("TRN2", target_bir_lowering=False, num_devices=1)
    arrays, io = {}, {}
    for short, name in NAMES.items():
        a = np.ascontiguousarray(inputs[name])
        arrays[f"in_{name}"] = a
        io[short] = nc.dram_tensor(f"in_{name}", a.shape, mybir.dt.from_np(a.dtype), kind="ExternalInput").ap()
    out = nc.dram_tensor("out_0", inputs["x"].shape, F32, kind="ExternalOutput").ap()
    build(nc, io, out, dve_chain=DVE_LINKS, pool_chain=POOL_LINKS)
    r = run(nc, [arrays], core_ids=[0])
    return r.results[0]["out_0"]
```

```python
from contextlib import ExitStack

import concourse.bass as bass
from concourse import mybir

F32 = mybir.dt.float32
ALU = mybir.AluOpType
ACT = mybir.ActivationFunctionType
AX = mybir.AxisListType

P = 128
SEQ = 64
D = 256
KC = D // P
SUB = 2
TOK = SUB * P
BPS = P // SEQ
NB = SUB * BPS
NSTREAM = 2
GROUPS = 8
HID = 1024
HC = HID // P
RING = 4

HEADS = {"S": 16, "C": 16, "G": 32}
JOINT = {a: HEADS[a] // GROUPS for a in "SCG"}
HD = {a: D // HEADS[a] for a in "SCG"}
PAIRW = {a: 2 * (HD[a] + 1) for a in "SCG"}
PAIRS = {a: HEADS[a] // 2 for a in "SCG"}
PT_JOBS = {a: PAIRS[a] // 4 for a in "SCG"}
VJOBS = {"S": 2, "C": 2, "G": 1}
EPS = {1: 1e-5, 2: 1e-5, 3: 1e-5, 4: 1e-6}


ORDER = """
QP1C' ET0 ST01 SA1C0' SC1C0' V1C' LN01 MX1C0' SA1C1' SC1C1' KP0S QP0S PT1C0' SA0S0 MX1C1' PO1C0'
SC0S0 PT1C1' KP1G' PO1C1' XB1C' SA0S1 CT1C' MX0S0 SC0S1 V0S PT0S0 MX0S1 OP1C' PO0S0 PT0S1 KP0C ST13'
PO0S1 CT0S XB0S LN13' OP0S ST02 H10' H13' XB1M' V0C LN02 GE10' XB0C H12' H11' QP0C GE13' SA0C0 GE12'
GE11' SC0C0 Y1' SA0C1 XT1' MX0C0 SC0C1 QP1G' PT0C0 SA1G0' MX0C1 KP0G SC1G0' PO0C0 V1G' SA1G1' PT0C1
MX1G0' SC1G1' PO0C1 PT1G0' CT0C XB1G' MX1G1' PO1G0' OP0C ST03 PT1G1' PO1G1' CT1G' V0G LN03 OP1G'
ST14' FN1' ST11 H01 H02 H00 ET1 LN11 H03 GE00 GE03 GE01 KP1S QP1S GE02 V1S SA1S0 XB0M SC1S0 Y0 SA1S1
XT0 XB1S MX1S0 SC1S1 QP0G PT1S0 SA0G0 MX1S1 SC0G0 KP1C MX0G0 PO1S0 SA0G1 SC0G1 PT1S1 PT0G0 MX0G1
PO1S1 PO0G0 CT1S PT0G1 OP1S ST12 PO0G1 XB0G CT0G LN12 OP0G ST04 FN0
""".split()


def parse(word):
    word, lag = word.rstrip("'"), int(word.endswith("'"))
    letters = 2 if word[1].isalpha() else 1
    return (word[:letters], *(int(c) if c.isdigit() else c for c in word[letters:])), lag


BODY = [parse(word) for word in ORDER]
HEAD = [(step, lag) for step, lag in BODY if not lag]
TAIL = [(step, lag) for step, lag in BODY if lag]
PROGRAM = {s: [step for step, lag in HEAD + TAIL if step[1] == s] for s in range(NSTREAM)}


def jobs_of(step):
    kind = step[0]
    if kind in ("ET", "LN", "XT", "CT"):
        return [("turn", "act")]
    if kind in ("QP", "KP"):
        return [("proj", "act")]
    if kind == "V":
        return [(f"v{n}", "act") for n in range(VJOBS[step[2]])]
    if kind == "PT":
        return [(f"p{n}", "act") for n in range(PT_JOBS[step[2]])]
    if kind == "PO":
        return [("o", "dve")]
    if kind == "H":
        return [("h", "act")]
    if kind in ("OP", "Y"):
        return [("out", "dve")]
    return []


def jobs_in(section):
    return [(step, job, lag, taker) for step, lag in section for job, taker in jobs_of(step)]


SECTIONS = {"head": HEAD, "body": BODY, "tail": TAIL}
JOBS = {name: jobs_in(section) for name, section in SECTIONS.items()}
SCORES = {name: [entry for entry in section if entry[0][0] == "SC"] for name, section in SECTIONS.items()}
BANK = {(step, job): n % RING for n, (step, job, _, _) in enumerate(JOBS["body"])}
DVE_LINKS = {"ST": 1, "MX": 1, "PO": 1, "H": 1}
POOL_LINKS = {"ST": 1, "FN": 1}
DVE_READY = 5


class Signal:

    def __init__(self, sem, events, unit=1):
        self.sem, self.events, self.unit = sem, list(events), unit
        self.worth = len(self.events) * unit

    def now(self, event, tile):
        return tile * self.worth + (self.worth + (self.events.index(event) + 1) * self.unit)

    def before(self, event, tile):
        return tile * self.worth + (self.events.index(event) + 1) * self.unit


def build(nc, io, out):
    turns = io["x"].shape[0] * SEQ // (NSTREAM * TOK)

    with ExitStack() as ctx:
        def sb(name, *free):
            return ctx.enter_context(nc.sbuf_tensor(name, [P, *free], F32))

        def psum(name, *free):
            return ctx.enter_context(nc.psum_tensor(name, [P, *free], F32))

        def sem(name):
            return ctx.enter_context(nc.semaphore(name))

        w_qkv = sb("w_qkv", KC, 3 * D)
        w_ao = sb("w_ao", KC, D)
        w_q = sb("w_q", KC, D)
        w_kv = sb("w_kv", KC, 2 * D)
        w_co = sb("w_co", KC, D)
        w_1 = sb("w_1", KC, HID)
        w_2 = sb("w_2", HC, D)
        g_q = sb("g_q", KC, D)
        g_kn = sb("g_kn", KC, 64)
        g_k = sb("g_k", KC, D)
        g_v = sb("g_v", KC, 64)
        g_o = sb("g_o", KC, D)
        w_of = {"S": (w_qkv[:, :, 0:D], w_qkv[:, :, D:2 * D], w_qkv[:, :, 2 * D:3 * D], w_ao),
                "C": (w_q, w_kv[:, :, 0:D], w_kv[:, :, D:2 * D], w_co),
                "G": (g_q, g_k, g_v, g_o)}
        col_ln = {n: (sb(f"ln{n}_s", KC), sb(f"ln{n}_b", KC)) for n in (1, 2, 3)}
        col_q = {a: sb(f"bias_q_{a}", KC) for a in "SCG"}
        col_k = {a: sb(f"bias_k_{a}", KC) for a in "SCG"}
        col_1 = sb("bias_1", HC)
        kmask = {a: sb(f"bias_k_masked_{a}", KC, JOINT[a]) for a in "SCG"}
        row_kn = sb("row_kn", 64)
        row_vn = sb("row_vn", 64)
        row_k = sb("row_k", D)
        row_v = {a: sb(f"row_v_{a}", D) for a in "SCG"}
        vspread = sb("vspread", KC, P)
        row_o = {a: sb(f"bias_o_{a}", D) for a in "SCMG"}
        gamma = sb("gamma", D)
        beta = sb("beta", D)
        ident = sb("ident", P)
        ones1 = sb("ones1", P)
        neghalf = sb("neghalf", SUB)
        onehot = {2: sb("onehot2", 4, 2), 4: sb("onehot4", 4, 4)}
        headmask = {2: sb("headmask2", 2), 4: sb("headmask4", 4)}
        mask_s = sb("mask_s", SEQ)
        off_s = sb("off_s", SEQ)

        both = range(NSTREAM)
        xin = [sb(f"xin{s}", SUB, D) for s in both]
        ein = [sb(f"ein{s}", SUB, D) for s in both]
        mask_c = [sb(f"mask_c{s}", SUB, SEQ) for s in both]
        off_c = [sb(f"off_c{s}", SUB, SEQ) for s in both]
        mask_g = [sb(f"mask_g{s}", SUB, SEQ) for s in both]
        xr = [sb(f"xr{s}", SUB, D) for s in both]
        xb = [sb(f"xb{s}", SUB, D) for s in both]
        z = [sb(f"z{s}", SUB, D) for s in both]
        stats = [sb(f"stats{s}", SUB, 6) for s in both]
        mv = [sb(f"mv{s}", SUB, 2) for s in both]
        veps = [sb(f"veps{s}", SUB) for s in both]
        rstd = [sb(f"rstd{s}", SUB) for s in both]
        zT = [sb(f"zT{s}", KC, TOK) for s in both]
        eT = [sb(f"eT{s}", KC, TOK) for s in both]
        qT = [sb(f"qT{s}", KC, TOK) for s in both]
        kbd = [sb(f"kbd{s}", KC, 4, TOK) for s in both]
        vb = {"L": [sb(f"vb{s}", NB, GROUPS, PAIRW["S"]) for s in both],
              "G": [sb(f"vg{s}", NB, GROUPS, PAIRW["G"]) for s in both]}
        attn_rows = [sb(f"attn{s}", SUB, D) for s in both]
        cT = [sb(f"cT{s}", KC, TOK) for s in both]
        res = [sb(f"res{s}", SUB, D) for s in both]
        su = [[sb(f"su{s}{t}", 2048) for t in range(SUB)] for s in both]
        pT = [sb(f"pT{s}", 2048) for s in both]
        mx = [sb(f"mx{s}", SUB, 32) for s in both]
        rden = [sb(f"rden{s}", SUB, 32) for s in both]

        scores = psum("scores", 4, 512)
        ring = [psum(f"ring{n}", 512) for n in range(RING)]

        s_w1st = sem("weights_self_loaded")
        s_wrest = sem("weights_rest_loaded")
        s_small = sem("small_loaded")
        s_const = sem("constants_made")
        s_turned = sem("biases_turned")
        s_prep = sem("operands_prepared")
        s_pre = sem("prologue_chain")
        s_prepool = sem("prologue_pool_chain")
        s_stand = sem("waits_met")

        def once(s):
            return [("tile", s)]

        def signal(name, events_of, unit=1):
            return [Signal(sem(f"{name}{s}"), events_of(s), unit) for s in both]

        def steps_of(*kinds):
            return lambda s: [step for step in PROGRAM[s] if step[0] in kinds]

        def jobs_for(*takers):
            return lambda s: [(step, job) for step in PROGRAM[s] for job, taker in jobs_of(step) if taker in takers]

        def links(count):
            return lambda s: [(step, n) for step in PROGRAM[s] for n in range(count.get(step[0], 0))]

        x_loaded = signal("x_loaded", once, 16)
        e_loaded = signal("e_loaded", once, 16)
        mc_loaded = signal("mask_c_loaded", once, 16)
        mg_loaded = signal("mask_g_loaded", once, 16)
        stored = signal("stored", once, 16)
        filled = signal("bank_filled", jobs_for("act", "dve"))
        by_act = signal("bank_emptied_by_act", jobs_for("act"))
        by_dve = signal("bank_emptied_by_dve", jobs_for("dve"))
        scored = signal("scores_filled", steps_of("SC"))
        masked = signal("scores_masked", steps_of("SC"))
        offset = signal("mask_offset_added", lambda s: [st for st in steps_of("SC")(s) if st[2] != "G"])
        shifted = signal("row_max_subtracted", steps_of("MX"))
        probs = signal("probs_ready", steps_of("MX"))
        moments = signal("moments_ready", steps_of("ST"))
        scaled = signal("rstd_ready", steps_of("ST"))
        normed = signal("normed_ready", steps_of("LN", "FN"))
        biased = signal("residual_biased", steps_of("XB"))
        offmask = signal("cross_offset_ready", once)
        cubic = signal("gelu_argument_ready", steps_of("H"))
        tanhed = signal("gelu_tanh_ready", steps_of("GE"))
        gelued = signal("gelu_ready", steps_of("GE"))
        finished = signal("result_ready", steps_of("FN"))
        dve_link = signal("dve_to_itself", links(DVE_LINKS))
        pool_link = signal("pool_to_itself", links(POOL_LINKS))

        def credit(eng, *signals):
            for per_stream in signals:
                for one in per_stream:
                    eng.sem_inc(one.sem, one.worth)

        def stream_of(event):
            return event[0][1] if isinstance(event[0], tuple) else event[1]

        def latest(signal, events):
            return max(events, key=signal[stream_of(events[0])].events.index)

        def wait(eng, signal, event, tile):
            one = signal[stream_of(event)]
            eng.wait_ge(one.sem, one.now(event, tile))

        def wait_before(eng, signal, event, tile):
            one = signal[stream_of(event)]
            eng.wait_ge(one.sem, one.before(event, tile))

        def last_user(users, section, n, same):
            for m in range(n - 1, -1, -1):
                if same(users[section][m]):
                    return users[section][m], 0
            if section == "head":
                return None, 0
            return [u for u in users["body"] if same(u)][-1], 1

        def stand(eng):
            eng.sem_inc(s_stand, 1)

        def cross(a):
            return "G" if a == "G" else "L"

        def score_view(a):
            return scores[:, :, 0:KC * JOINT[a] * SEQ].rearrange("p i (h k) -> p i h k", k=SEQ)

        def su_view(s, a, t):
            return su[s][t][:, 0:HEADS[a] * SEQ]

        def rows(dram):
            return dram.rearrange("(k p) n -> p k n", p=P)

        def row_of(vec):
            return vec.rearrange("(a n) -> a n", a=1)

        def column_of(vec):
            return vec.rearrange("(c p) -> p c", p=P)

        def bank(step, job):
            return ring[BANK[(step, job)]]

        block = ctx.enter_context(nc.Block())

        @block.sync
        def _(sp):
            def tiles(dram):
                return dram.flatten_outer_dims().rearrange("(n t p) d -> n p t d", t=SUB, p=P)

            x_v, e_v, o_v = tiles(io["x"]), tiles(io["ctx"]), tiles(out)
            mc_v, mg_v = tiles(io["mask_c"]), tiles(io["mask_g"])

            def load(tile, dram, signal, s, it):
                sp.dma_start(tile[s][:], dram[it * NSTREAM + s]).then_inc(signal[s].sem, 16)

            def store(s, it):
                sp.dma_start(o_v[it * NSTREAM + (s - NSTREAM)], res[s][:]).then_inc(stored[s].sem, 16)

            load(ein, e_v, e_loaded, 0, 0)
            load(xin, x_v, x_loaded, 0, 0)
            for tile, name in ((w_qkv, "w_qkv"), (w_ao, "w_ao")):
                sp.dma_start(tile[:], rows(io[name])).then_inc(s_w1st, 16)
            load(mask_c, mc_v, mc_loaded, 0, 0)
            for tile, name in ((g_kn, "Wk"), (g_o, "Wo"), (w_co, "w_co"), (w_q, "w_q"), (w_kv, "w_kv"), (w_1, "w_1"),
                               (w_2, "w_2"), (g_q, "Wq"), (g_v, "Wv")):
                sp.dma_start(tile[:], rows(io[name])).then_inc(s_wrest, 16)
            load(mask_g, mg_v, mg_loaded, 0, 0)
            load(ein, e_v, e_loaded, 1, 0)
            load(xin, x_v, x_loaded, 1, 0)
            load(mask_c, mc_v, mc_loaded, 1, 0)
            load(mask_g, mg_v, mg_loaded, 1, 0)
            credit(sp, stored, x_loaded, e_loaded, mc_loaded, mg_loaded)
            with sp.Fori(1, turns) as it:
                for s in both:
                    wait_before(sp, filled, (("ET", s), "turn"), it)
                    stand(sp)
                    load(ein, e_v, e_loaded, s, it)
                    wait_before(sp, normed, ("LN", s, 1), it)
                    stand(sp)
                    wait_before(sp, biased, ("XB", s, "S"), it)
                    stand(sp)
                    load(xin, x_v, x_loaded, s, it)
                    wait_before(sp, masked, latest(masked, [("SC", s, "C", t) for t in range(SUB)]), it)
                    stand(sp)
                    wait_before(sp, offmask, ("tile", s), it)
                    stand(sp)
                    load(mask_c, mc_v, mc_loaded, s, it)
                for s in both:
                    wait_before(sp, masked, latest(masked, [("SC", s, "G", t) for t in range(SUB)]), it)
                    stand(sp)
                    load(mask_g, mg_v, mg_loaded, s, it)
                    wait_before(sp, finished, ("FN", s), it)
                    stand(sp)
                    store(s, it)
            for s in both:
                wait_before(sp, finished, ("FN", s), turns)
                store(s, turns)
            for s in both:
                sp.wait_ge(stored[s].sem, (turns + 1) * stored[s].worth)

        small = 0

        @block.scalar
        def _(act):
            nonlocal small
            for n in (1, 2, 3):
                for tile, name in zip(col_ln[n], (f"ln{n}_s", f"ln{n}_b")):
                    act.dma_start(tile[:], column_of(io[name]), allow_slow_non_contiguous=True).then_inc(s_small, 16)
                    small += 16
            cols = ((col_q["S"], io["b_qkv"][0:D]), (col_k["S"], io["b_qkv"][D:2 * D]), (col_q["C"], io["b_q"]),
                    (col_k["C"], io["b_kv"][0:D]), (col_q["G"], io["bq"]), (col_1, io["b1"]))
            for tile, src in cols:
                act.dma_start(tile[:], column_of(src), allow_slow_non_contiguous=True).then_inc(s_small, 16)
                small += 16
            spread = ((row_o["S"], io["b_ao"]), (row_o["C"], io["b_co"]), (row_o["M"], io["b2"]),
                      (row_o["G"], io["bo"]), (gamma, io["gamma"]), (beta, io["beta"]))
            for tile, src in spread:
                act.dma_start(tile[:], row_of(src).broadcast_to([P, src.shape[0]])).then_inc(s_small, 16)
                small += 16
            for tile, src in ((row_kn, io["bk"]), (row_vn, io["bv"]), (row_v["S"], io["b_qkv"][2 * D:3 * D]),
                              (row_v["C"], io["b_kv"][D:2 * D])):
                act.dma_start(tile[0:1, :], row_of(src)).then_inc(s_small, 16)
                small += 16
            for h in range(BPS):
                act.dma_start(mask_s[h * SEQ:(h + 1) * SEQ, :], io["mask_s"][0, 0]).then_inc(s_small, 16)
                small += 16
            credit(act, by_act, probs, tanhed)
            act.wait_ge(s_small, small)
            act.wait_ge(s_prep, DVE_READY)

            def empty_turned(step, dst, tile, n=None):
                s = step[1]
                wait(act, filled, (step, "turn"), tile)
                src = bank(step, "turn")[:].rearrange("p (k n) -> p k n", k=KC)
                if n is None:
                    nc.scalar.copy(dst[:], src).then_inc(by_act[s].sem, 1)
                    return
                for k in range(KC):
                    last = nc.scalar.activation(dst[:, k, :], src[:, k, :], ACT.Identity,
                                                bias=col_ln[n][1][:, k:k + 1], scale=col_ln[n][0][:, k:k + 1])
                last.then_inc(by_act[s].sem, 1)

            def take(section, it):
                for n_step, (step, lag) in enumerate(SECTIONS[section]):
                    kind, s, tile = step[0], step[1], it - lag if lag else it
                    if kind == "ET":
                        empty_turned(step, eT[s], tile)
                    elif kind == "LN":
                        empty_turned(step, zT[s], tile, step[2])
                    elif kind == "XT":
                        empty_turned(step, zT[s], tile)
                    elif kind == "CT":
                        empty_turned(step, cT[s], tile)
                    elif kind == "QP":
                        a = step[2]
                        wait(act, filled, (step, "proj"), tile)
                        src = bank(step, "proj")[:].rearrange("p (k n) -> p k n", k=KC)
                        for k in range(KC):
                            last = nc.scalar.activation(qT[s][:, k, :], src[:, k, :], ACT.Identity,
                                                        bias=col_q[a][:, k:k + 1], scale=HD[a] ** -0.5)
                        last.then_inc(by_act[s].sem, 1)
                    elif kind == "KP":
                        a = step[2]
                        wait(act, filled, (step, "proj"), tile)
                        src = bank(step, "proj")[:].rearrange("p (k n) -> p k n", k=KC)
                        for k in range(KC):
                            for j in range(JOINT[a]):
                                last = nc.scalar.activation(kbd[s][:, k, j, :], src[:, k, :], ACT.Identity,
                                                            bias=kmask[a][:, k, j:j + 1],
                                                            scale=headmask[JOINT[a]][:, j:j + 1])
                        last.then_inc(by_act[s].sem, 1)
                    elif kind == "V":
                        a = step[2]
                        v, w, per = vb[cross(a)][s], HD[a] + 1, NB // VJOBS[a]
                        for n in range(VJOBS[a]):
                            wait(act, filled, (step, f"v{n}"), tile)
                            for j in range(2):
                                half = slice(64 * j, 64 * j + 64)
                                src = bank(step, f"v{n}")[half, 0:per * (64 if a == "G" else D)]
                                if a == "G":
                                    src = src.rearrange("p (b h d) -> p b h d", b=per, d=HD[a])
                                else:
                                    src = src.rearrange("p (b h j d) -> p b h j d", b=per, j=2, d=HD[a])[:, :, :, j, :]
                                last = nc.scalar.copy(v[half, n * per:(n + 1) * per, :, w * j:w * j + w - 1], src)
                            last.then_inc(by_act[s].sem, 1)
                    elif kind == "MX":
                        a, t = step[2:]
                        wait(act, shifted, step, tile)
                        nc.scalar.activation(su_view(s, a, t), su_view(s, a, t), ACT.Exp).then_inc(probs[s].sem, 1)
                    elif kind == "PT":
                        a, t = step[2:]
                        for n in range(PT_JOBS[a]):
                            wait(act, filled, (step, f"p{n}"), tile)
                            nc.scalar.copy(pT[s][:, n * 512:(n + 1) * 512],
                                           bank(step, f"p{n}")[:]).then_inc(by_act[s].sem, 1)
                    elif kind == "H":
                        m = step[2]
                        wait(act, filled, (step, "h"), tile)
                        for k in range(2):
                            c, lo = 2 * m + k, (2 * m + k) * TOK
                            src = bank(step, "h")[:, k * TOK:(k + 1) * TOK]
                            nc.scalar.activation(su[s][0][:, lo:lo + TOK], src, ACT.Identity, bias=col_1[:, c:c + 1])
                            last = nc.scalar.activation(su[s][1][:, lo:lo + TOK], src, ACT.Square,
                                                        bias=col_1[:, c:c + 1])
                        last.then_inc(by_act[s].sem, 1)
                    elif kind == "GE":
                        m = step[2]
                        part = su[s][1][:, m * 512:(m + 1) * 512]
                        wait(act, cubic, ("H", s, m), tile)
                        nc.scalar.activation(part, part, ACT.Tanh, scale=0.7978845608028654).then_inc(tanhed[s].sem, 1)

            take("head", 0)
            with act.Fori(1, turns) as it:
                take("body", it)
            take("tail", turns)

        @block.gpsimd
        def _(pool):
            chain = [0]

            def pre(ins):
                chain[0] += 1
                ins.then_inc(s_prepool, 1)
                pool.wait_ge(s_prepool, chain[0])

            pre(pool.memset(ident[:], 0.0))
            pre(pool.affine_select(out=ident[:], in_=ident[:], compare_op=ALU.not_equal, fill=1.0, base=0,
                                   pattern=[[-1, P]], channel_multiplier=1))
            pre(pool.memset(ones1[:], 1.0))
            pre(pool.memset(neghalf[:], -0.5))
            for g in (2, 4):
                w = 32 // g
                m = onehot[g]
                pre(pool.memset(m[:], 1.0))
                pre(pool.affine_select(out=m[:], in_=m[:], compare_op=ALU.is_ge, fill=0.0, base=0,
                                       pattern=[[-32, 4], [-w, g]], channel_multiplier=1))
                pre(pool.affine_select(out=m[:], in_=m[:], compare_op=ALU.is_ge, fill=0.0, base=w - 1,
                                       pattern=[[32, 4], [w, g]], channel_multiplier=-1))
            pool.sem_inc(s_const, 1)
            credit(pool, offset, scaled, biased, offmask, finished, pool_link)
            pool.wait_ge(s_prep, DVE_READY)

            def take(section, it):
                for n_step, (step, lag) in enumerate(SECTIONS[section]):
                    kind, s, tile = step[0], step[1], it - lag if lag else it
                    links = [0]

                    def link(ins):
                        one = pool_link[s]
                        ins.then_inc(one.sem, 1)
                        pool.wait_ge(one.sem, one.now((step, links[0]), tile))
                        links[0] += 1

                    if kind == "XB":
                        a = step[2]
                        bias = row_o[a][:, :].unsqueeze(1).to_broadcast([P, SUB, D])
                        if a == "S":
                            wait(pool, x_loaded, ("tile", s), tile)
                            wait_before(pool, by_dve, (("OP", s, "G"), "out"), tile)
                        else:
                            made = {"C": ("OP", s, "S"), "M": ("OP", s, "C"), "G": ("Y", s)}[a]
                            wait(pool, by_dve, (made, "out"), tile)
                        pool.tensor_tensor(xb[s][:], (xin[s][:] if a == "S" else xr[s][:]), bias,
                                           ALU.add).then_inc(biased[s].sem, 1)
                        if a == "S":
                            wait(pool, mc_loaded, ("tile", s), tile)
                            stand(pool)
                            pool.tensor_scalar(off_c[s][:], mask_c[s][:], -1.0, 10000.0, ALU.add,
                                               ALU.mult).then_inc(offmask[s].sem, 1)
                    elif kind == "ST":
                        wait(pool, moments, step, tile)
                        stand(pool)
                        link(pool.tensor_scalar(veps[s][:], mv[s][:, :, 1], EPS[step[2]], 1.0, ALU.add, ALU.mult))
                        pool.tensor_tensor(rstd[s][:], veps[s][:], neghalf[:], ALU.pow).then_inc(scaled[s].sem, 1)
                    elif kind == "FN":
                        wait(pool, normed, step, tile)
                        link(pool.tensor_tensor(res[s][:], res[s][:],
                                                gamma[:, :].unsqueeze(1).to_broadcast([P, SUB, D]), ALU.mult))
                        pool.tensor_tensor(res[s][:], res[s][:], beta[:, :].unsqueeze(1).to_broadcast([P, SUB, D]),
                                           ALU.add).then_inc(finished[s].sem, 1)
                    elif kind == "SC" and step[2] != "G":
                        a, t = step[2:]
                        off = off_s[:, :] if a == "S" else off_c[s][:, t]
                        if a == "C":
                            wait(pool, offmask, ("tile", s), tile)
                        wait(pool, masked, step, tile)
                        v = su_view(s, a, t).rearrange("p (h k) -> p h k", k=SEQ)
                        pool.tensor_tensor(v, v, off.unsqueeze(1).to_broadcast([P, HEADS[a], SEQ]),
                                           ALU.add).then_inc(offset[s].sem, 1)

            take("head", 0)
            with pool.Fori(1, turns) as it:
                take("body", it)
            take("tail", turns)

        @block.vector
        def _(dve):
            chain = [0]

            def pre(ins):
                chain[0] += 1
                ins.then_inc(s_pre, 1)
                dve.wait_ge(s_pre, chain[0])

            for s in both:
                for key, a in (("L", "S"), ("G", "G")):
                    v, w = vb[key][s], HD[a] + 1
                    pre(dve.memset(v[:], 0.0))
                    for j in range(2):
                        pre(dve.memset(v[64 * j:64 * j + 64, :, :, w * j + w - 1:w * j + w], 1.0))
            dve.wait_ge(s_small, small)
            pre(dve.tensor_scalar(off_s[:], mask_s[:], -1.0, 10000.0, ALU.add, ALU.mult))
            for a in "SCG":
                pre(dve.tensor_scalar(col_q[a][:], col_q[a][:], HD[a] ** -0.5, None, ALU.mult))
            for row, stored_row in ((row_k, row_kn), (row_v["G"], row_vn)):
                pre(dve.tensor_copy(row[0:1, :].rearrange("p (h g d) -> p h g d", g=4, d=8),
                                    stored_row[0:1, :].rearrange("p (h d) -> p h d", d=8).unsqueeze(2)
                                    .to_broadcast([1, 8, 4, 8])))
            dve.wait_ge(s_const, 1)
            dve.wait_ge(s_prepool, 10)
            for g in (2, 4):
                pre(dve.tensor_reduce(headmask[g][:], onehot[g][:].rearrange("p i j -> p j i"), AX.X, ALU.add))
            dve.sem_inc(s_prep, 1)
            dve.wait_ge(s_turned, 1)
            pre(dve.tensor_copy(col_k["G"][:], ring[0][:, 0:KC]))
            for a in "SCG":
                pre(dve.tensor_tensor(kmask[a][:], col_k[a][:, :].unsqueeze(2).to_broadcast([P, KC, JOINT[a]]),
                                      headmask[JOINT[a]][:, :].unsqueeze(1).to_broadcast([P, KC, JOINT[a]]), ALU.mult))
            dve.wait_ge(s_wrest, 16 * 9)
            for k in range(KC):
                pre(dve.tensor_copy(g_k[:, k, :].rearrange("p (h g d) -> p h g d", g=4, d=8),
                                    g_kn[:, k, :].rearrange("p (h d) -> p h d", d=8).unsqueeze(2)
                                    .to_broadcast([P, 8, 4, 8])))
            for n, a in enumerate("SCG"):
                dve.wait_ge(s_turned, 2 + 2 * n)
                pre(dve.tensor_copy(vspread[:].rearrange("p k n -> p (k n)"), ring[1][:, 0:KC * P]))
                dve.sem_inc(s_prep, 1)
                dve.wait_ge(s_turned, 3 + 2 * n)
                pre(dve.tensor_tensor(row_o[a][:], row_o[a][:], ring[2][:, 0:D], ALU.add))
            dve.sem_inc(s_prep, 1)
            credit(dve, by_dve, masked, shifted, moments, normed, cubic, gelued, dve_link)

            def take(section, it):
                for n_step, (step, lag) in enumerate(SECTIONS[section]):
                    kind, s, tile = step[0], step[1], it - lag if lag else it
                    links = [0]

                    def link(ins):
                        one = dve_link[s]
                        ins.then_inc(one.sem, 1)
                        dve.wait_ge(one.sem, one.now((step, links[0]), tile))
                        links[0] += 1

                    if kind == "ST":
                        if step[2] == 1:
                            wait(dve, x_loaded, ("tile", s), tile)
                        src = xin[s] if step[2] == 1 else xr[s]
                        for t in range(SUB):
                            last = dve.bn_stats(stats[s][:, t, :], src[:, t, :])
                        link(last)
                        stand(dve)
                        for t in range(SUB):
                            last = dve.bn_aggr(mv[s][:, t, :], stats[s][:, t, :])
                        last.then_inc(moments[s].sem, 1)
                    elif kind in ("LN", "FN"):
                        n = 4 if kind == "FN" else step[2]
                        src, dst = (xin[s] if n == 1 else xr[s]), (res[s] if n == 4 else z[s])
                        wait(dve, scaled, ("ST", s, n), tile)
                        if n == 4:
                            wait_before(dve, stored, ("tile", s), tile)
                        for t in range(SUB):
                            last = dve.tensor_scalar(dst[:, t, :], src[:, t, :], mv[s][:, t, 0:1],
                                                     rstd[s][:, t:t + 1], ALU.subtract, ALU.mult)
                        last.then_inc(normed[s].sem, 1)
                    elif kind == "SC":
                        a, t = step[2:]
                        m = {"S": mask_s[:, :], "C": mask_c[s][:, t], "G": mask_g[s][:, t]}[a]
                        if a == "C":
                            wait(dve, mc_loaded, ("tile", s), tile)
                        if a == "G":
                            wait(dve, mg_loaded, ("tile", s), tile)
                        wait(dve, scored, step, tile)
                        h = HEADS[a] // 4
                        dve.tensor_tensor(su_view(s, a, t).rearrange("p (i h k) -> p i h k", i=4, k=SEQ), score_view(a),
                                          m.unsqueeze(1).unsqueeze(1).to_broadcast([P, 4, h, SEQ]),
                                          ALU.add if a == "G" else ALU.mult).then_inc(masked[s].sem, 1)
                    elif kind == "MX":
                        a, t = step[2:]
                        if a == "G":
                            wait(dve, masked, ("SC", *step[1:]), tile)
                        else:
                            wait(dve, offset, ("SC", *step[1:]), tile)
                        v = su_view(s, a, t).rearrange("p (h k) -> p h k", k=SEQ)
                        top = mx[s][:, t, 0:HEADS[a]]
                        link(dve.tensor_reduce(top, v, AX.X, ALU.max))
                        dve.tensor_tensor(v, v, top.unsqueeze(2).to_broadcast([P, HEADS[a], SEQ]),
                                          ALU.subtract).then_inc(shifted[s].sem, 1)
                    elif kind == "PO":
                        a, t = step[2:]
                        n, w = HEADS[a], HD[a] + 1
                        wait(dve, filled, (step, "o"), tile)
                        o = bank(step, "o")[:, 0:n * w].rearrange("p (h d) -> p h d", d=w)
                        link(dve.reciprocal(rden[s][:, t, 0:n], o[:, :, w - 1]))
                        dve.tensor_tensor(attn_rows[s][:, t, :].rearrange("p (h d) -> p h d", d=w - 1), o[:, :, 0:w - 1],
                                          rden[s][:, t, 0:n].unsqueeze(2).to_broadcast([P, n, w - 1]),
                                          ALU.mult).then_inc(by_dve[s].sem, 1)
                    elif kind == "OP":
                        wait(dve, biased, ("XB", *step[1:]), tile)
                        wait(dve, filled, (step, "out"), tile)
                        dve.tensor_tensor(xr[s][:].rearrange("p t d -> p (t d)"), bank(step, "out")[:],
                                          xb[s][:].rearrange("p t d -> p (t d)"), ALU.add).then_inc(by_dve[s].sem, 1)
                        wait(dve, by_dve, (step, "out"), tile)
                    elif kind == "Y":
                        wait(dve, biased, ("XB", s, "M"), tile)
                        wait(dve, filled, (step, "out"), tile)
                        dve.scalar_tensor_tensor(out=xr[s][:].rearrange("p t d -> p (t d)"),
                                                 in0=bank(step, "out")[:], scalar=0.5,
                                                 in1=xb[s][:].rearrange("p t d -> p (t d)"), op0=ALU.mult,
                                                 op1=ALU.add).then_inc(by_dve[s].sem, 1)
                    elif kind == "H":
                        m = step[2]
                        hid, sq = su[s][0][:, m * 512:(m + 1) * 512], su[s][1][:, m * 512:(m + 1) * 512]
                        wait(dve, by_act, (step, "h"), tile)
                        link(dve.tensor_scalar(sq, sq, 0.044715, 1.0, ALU.mult, ALU.add))
                        dve.tensor_tensor(sq, sq, hid, ALU.mult).then_inc(cubic[s].sem, 1)
                    elif kind == "GE":
                        m = step[2]
                        hid, th = su[s][0][:, m * 512:(m + 1) * 512], su[s][1][:, m * 512:(m + 1) * 512]
                        wait(dve, tanhed, step, tile)
                        dve.scalar_tensor_tensor(out=hid, in0=th, scalar=1.0, in1=hid, op0=ALU.add,
                                                 op1=ALU.mult).then_inc(gelued[s].sem, 1)

            take("head", 0)
            with dve.Fori(1, turns) as it:
                take("body", it)
            take("tail", turns)

        @block.tensor
        def _(pe):
            pe.wait_ge(s_prep, 1)
            for k in range(KC):
                last = nc.tensor.matmul(ring[0][:, k:k + 1], row_k[0:1, k * P:(k + 1) * P], ones1[0:1, 0:1],
                                        start=True, stop=True)
            last.then_inc(s_turned, 1)
            pe.wait_ge(s_w1st, 32)
            pe.wait_ge(s_wrest, 16 * 9)
            for n, a in enumerate("SCG"):
                if n:
                    pe.wait_ge(s_prep, 1 + n)
                for k in range(KC):
                    last = nc.tensor.matmul(ring[1][:, k * P:(k + 1) * P], row_v[a][0:1, k * P:(k + 1) * P],
                                            ones1[0:1, :], start=True, stop=True)
                last.then_inc(s_turned, 1)
                pe.wait_ge(s_prep, 2 + n)
                for k in range(KC):
                    last = nc.tensor.matmul(ring[2][:, 0:D], vspread[:, k, :], w_of[a][3][:, k, :],
                                            start=(k == 0), stop=(k == KC - 1))
                last.then_inc(s_turned, 1)
            pe.wait_ge(s_prep, DVE_READY)
            credit(pe, filled, scored)

            def claim(section, n_step, job, it, known=None):
                step, lag = SECTIONS[section][n_step]
                n = [u[:2] for u in JOBS[section]].index((step, job))
                user, back = last_user(JOBS, section, n, lambda u: BANK[u[:2]] == BANK[(step, job)])
                if user:
                    signal, ago = (by_act if user[3] == "act" else by_dve), user[2] + back
                    if known and known[0] is signal and user[0][1] == step[1]:
                        events = signal[step[1]].events
                        if ago > lag or events.index(user[:2]) <= events.index(known[1]):
                            return bank(step, job)
                        stand(pe)
                    wait(pe, signal, user[:2], it - ago if ago else it)
                return bank(step, job)

            def turn_rows(step, src, b):
                s = step[1]
                for k in range(KC):
                    for t in range(SUB):
                        last = nc.tensor.transpose(b[:, k * TOK + t * P:k * TOK + (t + 1) * P],
                                                   src[:, t, k * P:(k + 1) * P], ident[:])
                last.then_inc(filled[s].sem, 1)

            def project_cols(step, b, w, src, m0=0):
                s = step[1]
                for m in range(2):
                    for k in range(KC):
                        last = nc.tensor.matmul(b[:, m * TOK:(m + 1) * TOK], w[:, k, (m0 + m) * P:(m0 + m + 1) * P],
                                                src[:, k, :], start=(k == 0), stop=(k == KC - 1))
                last.then_inc(filled[s].sem, 1)

            def score_chunk(a, s, t, k):
                g = JOINT[a]
                for flip in range(2):
                    for i in range(4):
                        b = (i + flip) % 2
                        r, tok = slice(32 * i, 32 * i + 32), t * P + b * SEQ
                        dst = scores[64 * b:64 * b + 64, i, k * g * SEQ:(k + 1) * g * SEQ]
                        last = nc.tensor.matmul(dst.rearrange("p (j k) -> p j k", k=SEQ),
                                                qT[s][r, k, tok:tok + SEQ], kbd[s][r, k, 0:g, tok:tok + SEQ],
                                                start=True, stop=True)
                return last

            def take(section, it):
                for n_step, (step, lag) in enumerate(SECTIONS[section]):
                    kind, s, tile = step[0], step[1], it - lag if lag else it
                    if kind == "ET":
                        wait(pe, e_loaded, ("tile", s), tile)
                        turn_rows(step, ein[s], claim(section, n_step, "turn", it))
                    elif kind == "LN":
                        wait(pe, normed, step, tile)
                        turn_rows(step, z[s], claim(section, n_step, "turn", it))
                    elif kind == "XT":
                        known = by_dve, (("Y", s), "out")
                        wait(pe, *known, tile)
                        turn_rows(step, xr[s], claim(section, n_step, "turn", it, known))
                    elif kind == "CT":
                        known = by_dve, latest(by_dve, [(("PO", s, step[2], t), "o") for t in range(SUB)])
                        wait(pe, *known, tile)
                        turn_rows(step, attn_rows[s], claim(section, n_step, "turn", it, known))
                    elif kind == "QP":
                        a = step[2]
                        known = by_act, ({"S": ("LN", s, 1), "C": ("LN", s, 2), "G": ("XT", s)}[a], "turn")
                        wait(pe, *known, tile)
                        project_cols(step, claim(section, n_step, "proj", it, known), w_of[a][0], zT[s])
                    elif kind == "KP":
                        a = step[2]
                        known = by_act, (("LN", s, 1) if a == "S" else ("ET", s), "turn")
                        wait(pe, *known, tile)
                        project_cols(step, claim(section, n_step, "proj", it, known), w_of[a][1], zT[s] if a == "S" else eT[s])
                    elif kind == "V":
                        a = step[2]
                        src, w, width = (zT[s] if a == "S" else eT[s]), w_of[a][2], (64 if a == "G" else D)
                        per = NB // VJOBS[a]
                        known = by_act, (("LN", s, 1) if a == "S" else ("ET", s), "turn")
                        wait(pe, *known, tile)
                        for n in range(VJOBS[a]):
                            b = claim(section, n_step, f"v{n}", it, known)
                            for q in range(per):
                                seq = n * per + q
                                for k in range(KC):
                                    for j in range(2):
                                        last = nc.tensor.matmul(b[64 * j:64 * j + 64, q * width:(q + 1) * width],
                                                                src[:, k, seq * SEQ:(seq + 1) * SEQ], w[:, k, :],
                                                                start=(k == 0), stop=(k == KC - 1))
                            last.then_inc(filled[s].sem, 1)
                    elif kind == "SA":
                        a, t = step[2:]
                        wait(pe, by_act, latest(by_act, [(("QP", s, a), "proj"), (("KP", s, a), "proj")]), tile)
                        n = [u[0] for u in SCORES[section]].index(("SC", *step[1:]))
                        user, back = last_user(SCORES, section, n, lambda u: True)
                        if user:
                            ago = user[1] + back
                            wait(pe, masked, user[0], it - ago if ago else it)
                        score_chunk(a, s, t, 0)
                    elif kind == "SC":
                        a, t = step[2:]
                        score_chunk(a, s, t, 1).then_inc(scored[s].sem, 1)
                    elif kind == "PT":
                        a, t = step[2:]
                        wait(pe, probs, ("MX", *step[1:]), tile)
                        for n in range(PT_JOBS[a]):
                            b = claim(section, n_step, f"p{n}", it)
                            for c in range(4):
                                lo = (4 * n + c) * P
                                last = nc.tensor.transpose(b[:, c * P:(c + 1) * P], su[s][t][:, lo:lo + P], ident[:])
                            last.then_inc(filled[s].sem, 1)
                    elif kind == "PO":
                        a, t = step[2:]
                        known = by_act, latest(by_act, [(("PT", *step[1:]), f"p{PT_JOBS[a] - 1}"),
                                                        (("V", s, a), f"v{VJOBS[a] - 1}")])
                        wait(pe, *known, tile)
                        b = claim(section, n_step, "o", it, known)
                        g2, w = JOINT[a] // 2, PAIRW[a]
                        for pair in range(PAIRS[a]):
                            i, k, jj = pair // (KC * g2), pair // g2 % KC, pair % g2
                            group = 4 * k + i
                            at = (group * g2 + jj) * w
                            for q in range(BPS):
                                last = nc.tensor.matmul(b[64 * q:64 * q + 64, at:at + w],
                                                        pT[s][:, pair * P + q * SEQ:pair * P + (q + 1) * SEQ],
                                                        vb[cross(a)][s][:, t * BPS + q, group, :], start=True, stop=True)
                        last.then_inc(filled[s].sem, 1)
                    elif kind == "OP":
                        known = by_act, (("CT", *step[1:]), "turn")
                        wait(pe, *known, tile)
                        b = claim(section, n_step, "out", it, known)
                        for t in range(SUB):
                            for k in range(KC):
                                last = nc.tensor.matmul(b[:, t * D:(t + 1) * D], cT[s][:, k, t * P:(t + 1) * P],
                                                        w_of[step[2]][3][:, k, :], start=(k == 0), stop=(k == KC - 1))
                        last.then_inc(filled[s].sem, 1)
                    elif kind == "H":
                        known = by_act, (("LN", s, 3), "turn")
                        wait(pe, *known, tile)
                        project_cols(step, claim(section, n_step, "h", it, known), w_1, zT[s], 2 * step[2])
                    elif kind == "Y":
                        wait(pe, gelued, latest(gelued, [("GE", s, m) for m in range(HC // 2)]), tile)
                        b = claim(section, n_step, "out", it)
                        for t in range(SUB):
                            for m in range(HC):
                                lo = m * TOK + t * P
                                last = nc.tensor.matmul(b[:, t * D:(t + 1) * D], su[s][0][:, lo:lo + P], w_2[:, m, :],
                                                        start=(m == 0), stop=(m == HC - 1))
                        last.then_inc(filled[s].sem, 1)

            take("head", 0)
            with pe.Fori(1, turns) as it:
                take("body", it)
            take("tail", turns)


NAMES = {"x": "x", "ctx": "ctx_2048", "mask_s": "mask_1x1xSxS2_fc1", "mask_c": "mask_Bx1xSxS2_ff1",
         "mask_g": "mask_Bx1xSxS2_ff0",
         **{n: f"L0_xattn_{n}" for n in ("ln1_s", "ln1_b", "w_qkv", "b_qkv", "w_ao", "b_ao", "ln2_s", "ln2_b", "w_q",
                                         "b_q", "w_kv", "b_kv", "w_co", "b_co", "ln3_s", "ln3_b", "b1", "b2")},
         "w_1": "L0_xattn_w1", "w_2": "L0_xattn_w2",
         **{n: f"L1_xattn_{n}" for n in ("Wq", "bq", "Wk", "bk", "Wv", "bv", "Wo", "bo", "gamma", "beta")}}


def kernel(**inputs):
    import numpy as np
    import concourse.bacc as bacc
    from concourse.bass_utils import run_bass_kernel_spmd as run

    nc = bacc.Bacc("TRN2", target_bir_lowering=False, num_devices=1)
    arrays, io = {}, {}
    for short, name in NAMES.items():
        a = np.ascontiguousarray(inputs[name])
        arrays[f"in_{name}"] = a
        io[short] = nc.dram_tensor(f"in_{name}", a.shape, mybir.dt.from_np(a.dtype), kind="ExternalInput").ap()
    out = nc.dram_tensor("out_0", inputs["x"].shape, F32, kind="ExternalOutput").ap()
    build(nc, io, out)
    r = run(nc, [arrays], core_ids=[0])
    return r.results[0]["out_0"]
```

```python
from contextlib import ExitStack

import concourse.bass as bass
from concourse import mybir

F32 = mybir.dt.float32
ALU = mybir.AluOpType
ACT = mybir.ActivationFunctionType
AX = mybir.AxisListType

P = 128
SEQ = 64
D = 256
KC = D // P
SUB = 2
TOK = SUB * P
BPS = P // SEQ
NB = SUB * BPS
NSTREAM = 2
GROUPS = 8
HID = 1024
HC = HID // P
RING = 4

HEADS = {"S": 16, "C": 16, "G": 32}
JOINT = {a: HEADS[a] // GROUPS for a in "SCG"}
HD = {a: D // HEADS[a] for a in "SCG"}
PAIRW = {a: 2 * (HD[a] + 1) for a in "SCG"}
PAIRS = {a: HEADS[a] // 2 for a in "SCG"}
PT_JOBS = {a: PAIRS[a] // 4 for a in "SCG"}
EPS = {1: 1e-5, 2: 1e-5, 3: 1e-5, 4: 1e-6}


ORDER = """
ST01 ET0 SA1C0' SC1C0' V1C' SA1C1' LN01 XB1C' SC1C1' KP0S QP0S SA0S0 MX1C0' MX1C1' SC0S0 PT1C0' V0S
PO1C0' SA0S1 PT1C1' MX0S0 SC0S1 PO1C1' PT0S0 CT1C' MX0S1 PO0S0 OP1C' ST13' PT0S1 PO0S1 XB0S CT0S
LN13' OP0S V0C ST02 KP0C LN02 H10' XB1M' H12' H11' GE10' GE12' H13' QP0C GE11' GE13' KP1G' SA0C0
SC0C0 Y1' SA0C1 XT1' MX0C0 SC0C1 QP1G' SA1G0' SC1G0' PT0C0 KP0G MX0C1 V1G' SA1G1' MX1G0' PO0C0
SC1G1' PT0C1 PT1G0' XB0C MX1G1' PO0C1 PO1G0' CT0C PT1G1' OP0C ST03 PO1G1' XB1G' LN03 CT1G' V0G OP1G'
ST14' FN1' ST11 H01 H03 ET1 LN11 GE01 H02 KP1S GE02 XB1S QP1S H00 GE03 GE00 XB0M SA1S0 V1S SC1S0
MX1S0 Y0 SA1S1 SC1S1 XT0 PT1S0 QP0G PO1S0 MX1S1 SA0G0 SC0G0 KP1C SA0G1 MX0G0 SC0G1 PT1S1 PT0G0 MX0G1
PO1S1 PO0G0 CT1S PT0G1 OP1S ST12 XB0G PO0G1 CT0G LN12 OP0G ST04 FN0 QP1C
""".split()


def parse(word):
    word, lag = word.rstrip("'"), int(word.endswith("'"))
    letters = 2 if word[1].isalpha() else 1
    return (word[:letters], *(int(c) if c.isdigit() else c for c in word[letters:])), lag


BODY = [parse(word) for word in ORDER]
HEAD = [(step, lag) for step, lag in BODY if not lag]
TAIL = [(step, lag) for step, lag in BODY if lag]
PROGRAM = {s: [step for step, lag in HEAD + TAIL if step[1] == s] for s in range(NSTREAM)}


def jobs_of(step):
    kind = step[0]
    if kind in ("ET", "LN", "XT", "CT"):
        return [("turn", "act")]
    if kind in ("QP", "KP"):
        return [("proj", "act")]
    if kind == "V":
        return [("v", "act")]
    if kind == "PT":
        return [(f"p{n}", "act") for n in range(PT_JOBS[step[2]])]
    if kind == "PO":
        return [("o", "dve")]
    if kind == "H":
        return [("h", "act")]
    if kind in ("OP", "Y"):
        return [("out", "dve")]
    return []


def jobs_in(section):
    return [(step, job, lag, taker) for step, lag in section for job, taker in jobs_of(step)]


SECTIONS = {"head": HEAD, "body": BODY, "tail": TAIL}
JOBS = {name: jobs_in(section) for name, section in SECTIONS.items()}
SCORES = {name: [entry for entry in section if entry[0][0] == "SC"] for name, section in SECTIONS.items()}
BANK = {(step, job): n % RING for n, (step, job, _, _) in enumerate(JOBS["body"])}
DVE_LINKS = {"ST": 1, "MX": 1, "PO": 1, "H": 1}
POOL_LINKS = {"ST": 1, "FN": 1}
DVE_READY = 3


class Signal:

    def __init__(self, sem, events, unit=1):
        self.sem, self.events, self.unit = sem, list(events), unit
        self.worth = len(self.events) * unit

    def now(self, event, tile):
        return tile * self.worth + (self.worth + (self.events.index(event) + 1) * self.unit)

    def before(self, event, tile):
        return tile * self.worth + (self.events.index(event) + 1) * self.unit


def build(nc, io, out):
    turns = io["x"].shape[0] * SEQ // (NSTREAM * TOK)

    with ExitStack() as ctx:
        def sb(name, *free):
            return ctx.enter_context(nc.sbuf_tensor(name, [P, *free], F32))

        def psum(name, *free):
            return ctx.enter_context(nc.psum_tensor(name, [P, *free], F32))

        def sem(name):
            return ctx.enter_context(nc.semaphore(name))

        w_qkv = sb("w_qkv", KC, 3 * D)
        w_ao = sb("w_ao", KC, D)
        w_q = sb("w_q", KC, D)
        w_kv = sb("w_kv", KC, 2 * D)
        w_co = sb("w_co", KC, D)
        w_1 = sb("w_1", KC, HID)
        w_2 = sb("w_2", HC, D)
        g_q = sb("g_q", KC, D)
        g_kn = sb("g_kn", KC, 64)
        g_k = sb("g_k", KC, D)
        g_v = sb("g_v", KC, 64)
        g_o = sb("g_o", KC, D)
        w_of = {"S": (w_qkv[:, :, 0:D], w_qkv[:, :, D:2 * D], w_qkv[:, :, 2 * D:3 * D], w_ao),
                "C": (w_q, w_kv[:, :, 0:D], w_kv[:, :, D:2 * D], w_co),
                "G": (g_q, g_k, g_v, g_o)}
        col_ln = {n: (sb(f"ln{n}_s", KC), sb(f"ln{n}_b", KC)) for n in (1, 2, 3)}
        col_q = {a: sb(f"bias_q_{a}", KC) for a in "SCG"}
        col_k = {a: sb(f"bias_k_{a}", KC) for a in "SCG"}
        col_1 = sb("bias_1", HC)
        kmask = {a: sb(f"bias_k_masked_{a}", KC, JOINT[a]) for a in "SCG"}
        row_kn = sb("row_kn", 64)
        row_vn = sb("row_vn", 64)
        row_k = sb("row_k", D)
        row_v = {a: sb(f"row_v_{a}", D) for a in "SCG"}
        vspread = {a: sb(f"vspread_{a}", KC, P) for a in "SCG"}
        row_o = {a: sb(f"bias_o_{a}", D) for a in "SCMG"}
        gamma = sb("gamma", D)
        beta = sb("beta", D)
        ident = sb("ident", P)
        ones1 = sb("ones1", P)
        neghalf = sb("neghalf", SUB)
        onehot = {2: sb("onehot2", 4, 2), 4: sb("onehot4", 4, 4)}
        headmask = {2: sb("headmask2", 2), 4: sb("headmask4", 4)}
        mask_s = sb("mask_s", SEQ)
        off_s = sb("off_s", SEQ)

        both = range(NSTREAM)
        xin = [sb(f"xin{s}", SUB, D) for s in both]
        ein = [sb(f"ein{s}", SUB, D) for s in both]
        mask_c = [sb(f"mask_c{s}", SUB, SEQ) for s in both]
        off_c = [sb(f"off_c{s}", SUB, SEQ) for s in both]
        mask_g = [sb(f"mask_g{s}", SUB, SEQ) for s in both]
        xr = [sb(f"xr{s}", SUB, D) for s in both]
        xb = [sb(f"xb{s}", SUB, D) for s in both]
        z = [sb(f"z{s}", SUB, D) for s in both]
        stats = [sb(f"stats{s}", SUB, 6) for s in both]
        mv = [sb(f"mv{s}", SUB, 2) for s in both]
        veps = [sb(f"veps{s}", SUB) for s in both]
        rstd = [sb(f"rstd{s}", SUB) for s in both]
        zT = [sb(f"zT{s}", KC, TOK) for s in both]
        eT = [sb(f"eT{s}", KC, TOK) for s in both]
        qT = [sb(f"qT{s}", KC, TOK) for s in both]
        kbd = [sb(f"kbd{s}", KC, 4, TOK) for s in both]
        vb = {"L": [sb(f"vb{s}", NB, GROUPS, PAIRW["S"]) for s in both],
              "G": [sb(f"vg{s}", NB, GROUPS, PAIRW["G"]) for s in both]}
        vcross = {"L": [sb(f"vcross_l{s}", SUB, GROUPS, PAIRW["S"]) for s in both],
                  "G": [sb(f"vcross_g{s}", SUB, GROUPS, PAIRW["G"]) for s in both]}
        attn_rows = [sb(f"attn{s}", SUB, D) for s in both]
        cT = [sb(f"cT{s}", KC, TOK) for s in both]
        res = [sb(f"res{s}", SUB, D) for s in both]
        su = [[sb(f"su{s}{t}", 2048) for t in range(SUB)] for s in both]
        pT = [sb(f"pT{s}", 2048) for s in both]
        mx = [sb(f"mx{s}", SUB, 32) for s in both]
        rden = [sb(f"rden{s}", SUB, 32) for s in both]

        scores = psum("scores", 4, 512)
        ring = [psum(f"ring{n}", 512) for n in range(RING)]

        s_w1st = sem("self_and_output_weights_loaded")
        s_wrest = sem("weights_rest_loaded")
        s_small = sem("small_loaded")
        s_rows = sem("key_and_value_bias_rows_loaded")
        s_const = sem("constants_made")
        s_turned = sem("biases_turned")
        s_prep = sem("operands_prepared")
        s_pre = sem("prologue_chain")
        s_prepool = sem("prologue_pool_chain")
        s_stand = sem("waits_met")

        def once(s):
            return [("tile", s)]

        def signal(name, events_of, unit=1):
            return [Signal(sem(f"{name}{s}"), events_of(s), unit) for s in both]

        def steps_of(*kinds):
            return lambda s: [step for step in PROGRAM[s] if step[0] in kinds]

        def jobs_for(*takers):
            return lambda s: [(step, job) for step in PROGRAM[s] for job, taker in jobs_of(step) if taker in takers]

        def links(count):
            return lambda s: [(step, n) for step in PROGRAM[s] for n in range(count.get(step[0], 0))]

        x_loaded = signal("x_loaded", once, 16)
        e_loaded = signal("e_loaded", once, 16)
        mc_loaded = signal("mask_c_loaded", once, 16)
        mg_loaded = signal("mask_g_loaded", once, 16)
        stored = signal("stored", once, 16)
        filled = signal("bank_filled", jobs_for("act", "dve"))
        by_act = signal("bank_emptied_by_act", jobs_for("act"))
        by_dve = signal("bank_emptied_by_dve", jobs_for("dve"))
        crossed = {key: signal(f"values_crossed_over_{key}", lambda s: [st for st in steps_of("V")(s) if st[2] in of], 32)
                   for key, of in (("L", "SC"), ("G", "G"))}
        scored = signal("scores_filled", steps_of("SC"))
        masked = signal("scores_masked", steps_of("SC"))
        offset = signal("mask_offset_added", lambda s: [st for st in steps_of("SC")(s) if st[2] != "G"])
        shifted = signal("row_max_subtracted", steps_of("MX"))
        probs = signal("probs_ready", steps_of("MX"))
        moments = signal("moments_ready", steps_of("ST"))
        scaled = signal("rstd_ready", steps_of("ST"))
        normed = signal("normed_ready", steps_of("LN", "FN"))
        biased = signal("residual_biased", steps_of("XB"))
        offmask = signal("cross_offset_ready", once)
        cubic = signal("gelu_argument_ready", steps_of("H"))
        tanhed = signal("gelu_tanh_ready", steps_of("GE"))
        gelued = signal("gelu_ready", steps_of("GE"))
        finished = signal("result_ready", steps_of("FN"))
        dve_link = signal("dve_to_itself", links(DVE_LINKS))
        pool_link = signal("pool_to_itself", links(POOL_LINKS))

        def credit(eng, *signals):
            for per_stream in signals:
                for one in per_stream:
                    eng.sem_inc(one.sem, one.worth)

        def stream_of(event):
            return event[0][1] if isinstance(event[0], tuple) else event[1]

        def latest(signal, events):
            return max(events, key=signal[stream_of(events[0])].events.index)

        def wait(eng, signal, event, tile):
            one = signal[stream_of(event)]
            eng.wait_ge(one.sem, one.now(event, tile))

        def wait_before(eng, signal, event, tile):
            one = signal[stream_of(event)]
            eng.wait_ge(one.sem, one.before(event, tile))

        def last_user(users, section, n, same):
            for m in range(n - 1, -1, -1):
                if same(users[section][m]):
                    return users[section][m], 0
            if section == "head":
                return None, 0
            return [u for u in users["body"] if same(u)][-1], 1

        def stand(eng):
            eng.sem_inc(s_stand, 1)

        def cross(a):
            return "G" if a == "G" else "L"

        def of_sequence(v, b):
            return v.rearrange("p (t b) g w -> p t b g w", b=BPS)[:, :, b]

        def score_view(a):
            return scores[:, :, 0:KC * JOINT[a] * SEQ].rearrange("p i (h k) -> p i h k", k=SEQ)

        def su_view(s, a, t):
            return su[s][t][:, 0:HEADS[a] * SEQ]

        def rows(dram):
            return dram.rearrange("(k p) n -> p k n", p=P)

        def row_of(vec):
            return vec.rearrange("(a n) -> a n", a=1)

        def column_of(vec):
            return vec.rearrange("(c p) -> p c", p=P)

        def bank(step, job):
            return ring[BANK[(step, job)]]

        block = ctx.enter_context(nc.Block())

        @block.sync
        def _(sp):
            def tiles(dram):
                return dram.flatten_outer_dims().rearrange("(n t p) d -> n p t d", t=SUB, p=P)

            x_v, e_v, o_v = tiles(io["x"]), tiles(io["ctx"]), tiles(out)
            mc_v, mg_v = tiles(io["mask_c"]), tiles(io["mask_g"])

            def load(tile, dram, signal, s, it):
                sp.dma_start(tile[s][:], dram[it * NSTREAM + s]).then_inc(signal[s].sem, 16)

            load(ein, e_v, e_loaded, 0, 0)
            load(xin, x_v, x_loaded, 0, 0)
            for tile, name in ((w_qkv, "w_qkv"), (w_ao, "w_ao"), (w_co, "w_co"), (g_o, "Wo")):
                sp.dma_start(tile[:], rows(io[name])).then_inc(s_w1st, 16)
            load(mask_c, mc_v, mc_loaded, 0, 0)
            for tile, name in ((g_kn, "Wk"), (w_q, "w_q"), (w_kv, "w_kv"), (w_1, "w_1"),
                               (w_2, "w_2"), (g_q, "Wq"), (g_v, "Wv")):
                sp.dma_start(tile[:], rows(io[name])).then_inc(s_wrest, 16)
            load(mask_g, mg_v, mg_loaded, 0, 0)
            load(ein, e_v, e_loaded, 1, 0)
            load(xin, x_v, x_loaded, 1, 0)
            load(mask_c, mc_v, mc_loaded, 1, 0)
            load(mask_g, mg_v, mg_loaded, 1, 0)
            credit(sp, stored, x_loaded, e_loaded, mc_loaded, mg_loaded, *crossed.values())

            def after(s, tile, *made):
                for signal, event in made:
                    wait(sp, signal, event, tile)
                    stand(sp)

            def take(section, it, last_turn=False):
                for step, lag in SECTIONS[section]:
                    kind, s, tile = step[0], step[1], it - lag if lag else it
                    follow = section != "tail" and not (last_turn and lag == 0)
                    if kind == "V":
                        a = step[2]
                        v, c = vb[cross(a)][s], vcross[cross(a)][s]
                        after(s, tile, (by_act, (step, "v")))
                        for b in range(BPS):
                            here, there = slice(SEQ * b, SEQ * b + SEQ), slice(SEQ - SEQ * b, P - SEQ * b)
                            sp.dma_start(of_sequence(v[there], b), c[here]).then_inc(crossed[cross(a)][s].sem, 16)
                    elif kind == "Y" and follow:
                        after(s, tile, (filled, (("ET", s), "turn")))
                        load(ein, e_v, e_loaded, s, tile + 1)
                        after(s, tile, (normed, ("LN", s, 1)), (biased, ("XB", s, "S")))
                        load(xin, x_v, x_loaded, s, tile + 1)
                        after(s, tile, (masked, latest(masked, [("SC", s, "C", t) for t in range(SUB)])),
                              (offmask, ("tile", s)))
                        load(mask_c, mc_v, mc_loaded, s, tile + 1)
                    elif kind == "FN":
                        after(s, tile, (finished, step))
                        sp.dma_start(o_v[tile * NSTREAM + s], res[s][:]).then_inc(stored[s].sem, 16)
                        if follow:
                            after(s, tile, (masked, latest(masked, [("SC", s, "G", t) for t in range(SUB)])))
                            load(mask_g, mg_v, mg_loaded, s, tile + 1)

            take("head", 0)
            with sp.Fori(1, turns - 1) as it:
                take("body", it)
            take("body", turns - 1, last_turn=True)
            take("tail", turns)
            for s in both:
                sp.wait_ge(stored[s].sem, (turns + 1) * stored[s].worth)

        small = 0

        @block.scalar
        def _(act):
            nonlocal small
            for tile, src in ((row_kn, io["bk"]), (row_vn, io["bv"]), (row_v["S"], io["b_qkv"][2 * D:3 * D]),
                              (row_v["C"], io["b_kv"][D:2 * D])):
                act.dma_start(tile[0:1, :], row_of(src)).then_inc(s_rows, 16)
            for n in (1, 2, 3):
                for tile, name in zip(col_ln[n], (f"ln{n}_s", f"ln{n}_b")):
                    act.dma_start(tile[:], column_of(io[name]), allow_slow_non_contiguous=True).then_inc(s_small, 16)
                    small += 16
            cols = ((col_q["S"], io["b_qkv"][0:D]), (col_k["S"], io["b_qkv"][D:2 * D]), (col_q["C"], io["b_q"]),
                    (col_k["C"], io["b_kv"][0:D]), (col_q["G"], io["bq"]), (col_1, io["b1"]))
            for tile, src in cols:
                act.dma_start(tile[:], column_of(src), allow_slow_non_contiguous=True).then_inc(s_small, 16)
                small += 16
            spread = ((row_o["S"], io["b_ao"]), (row_o["C"], io["b_co"]), (row_o["M"], io["b2"]),
                      (row_o["G"], io["bo"]), (gamma, io["gamma"]), (beta, io["beta"]))
            for tile, src in spread:
                act.dma_start(tile[:], row_of(src).broadcast_to([P, src.shape[0]])).then_inc(s_small, 16)
                small += 16
            for h in range(BPS):
                act.dma_start(mask_s[h * SEQ:(h + 1) * SEQ, :], io["mask_s"][0, 0]).then_inc(s_small, 16)
                small += 16
            credit(act, by_act, probs, tanhed)
            act.wait_ge(s_small, small)
            act.wait_ge(s_prep, DVE_READY)

            def empty_turned(step, dst, tile, n=None):
                s = step[1]
                wait(act, filled, (step, "turn"), tile)
                src = bank(step, "turn")[:].rearrange("p (k n) -> p k n", k=KC)
                if n is None:
                    nc.scalar.copy(dst[:], src).then_inc(by_act[s].sem, 1)
                    return
                for k in range(KC):
                    last = nc.scalar.activation(dst[:, k, :], src[:, k, :], ACT.Identity,
                                                bias=col_ln[n][1][:, k:k + 1], scale=col_ln[n][0][:, k:k + 1])
                last.then_inc(by_act[s].sem, 1)

            def take(section, it):
                for n_step, (step, lag) in enumerate(SECTIONS[section]):
                    kind, s, tile = step[0], step[1], it - lag if lag else it
                    if kind == "ET":
                        empty_turned(step, eT[s], tile)
                    elif kind == "LN":
                        empty_turned(step, zT[s], tile, step[2])
                    elif kind == "XT":
                        empty_turned(step, zT[s], tile)
                    elif kind == "CT":
                        empty_turned(step, cT[s], tile)
                    elif kind == "QP":
                        a = step[2]
                        wait(act, filled, (step, "proj"), tile)
                        src = bank(step, "proj")[:].rearrange("p (k n) -> p k n", k=KC)
                        for k in range(KC):
                            last = nc.scalar.activation(qT[s][:, k, :], src[:, k, :], ACT.Identity,
                                                        bias=col_q[a][:, k:k + 1], scale=HD[a] ** -0.5)
                        last.then_inc(by_act[s].sem, 1)
                    elif kind == "KP":
                        a = step[2]
                        wait(act, filled, (step, "proj"), tile)
                        src = bank(step, "proj")[:].rearrange("p (k n) -> p k n", k=KC)
                        for k in range(KC):
                            for j in range(JOINT[a]):
                                last = nc.scalar.activation(kbd[s][:, k, j, :], src[:, k, :], ACT.Identity,
                                                            bias=kmask[a][:, k, j:j + 1],
                                                            scale=headmask[JOINT[a]][:, j:j + 1])
                        last.then_inc(by_act[s].sem, 1)
                    elif kind == "V":
                        a = step[2]
                        v, c, w = vb[cross(a)][s], vcross[cross(a)][s], HD[a] + 1
                        wait(act, filled, (step, "v"), tile)
                        for b in range(BPS):
                            half = slice(SEQ * b, SEQ * b + SEQ)
                            for j in range(2):
                                src = bank(step, "v")[half, 0:SUB * (64 if a == "G" else D)]
                                if a == "G":
                                    src = src.rearrange("p (t h d) -> p t h d", t=SUB, d=HD[a])
                                else:
                                    src = src.rearrange("p (t h j d) -> p t h j d", t=SUB, j=2, d=HD[a])[:, :, :, j, :]
                                if j == b:
                                    dst = of_sequence(v[half], b)
                                else:
                                    dst = c[half]
                                last = nc.scalar.copy(dst[:, :, :, w * j:w * j + w - 1], src)
                        last.then_inc(by_act[s].sem, 1)
                    elif kind == "MX":
                        a, t = step[2:]
                        wait(act, shifted, step, tile)
                        nc.scalar.activation(su_view(s, a, t), su_view(s, a, t), ACT.Exp).then_inc(probs[s].sem, 1)
                    elif kind == "PT":
                        a, t = step[2:]
                        for n in range(PT_JOBS[a]):
                            wait(act, filled, (step, f"p{n}"), tile)
                            nc.scalar.copy(pT[s][:, n * 512:(n + 1) * 512],
                                           bank(step, f"p{n}")[:]).then_inc(by_act[s].sem, 1)
                    elif kind == "H":
                        m = step[2]
                        wait(act, filled, (step, "h"), tile)
                        for k in range(2):
                            c, lo = 2 * m + k, (2 * m + k) * TOK
                            src = bank(step, "h")[:, k * TOK:(k + 1) * TOK]
                            nc.scalar.activation(su[s][0][:, lo:lo + TOK], src, ACT.Identity, bias=col_1[:, c:c + 1])
                            last = nc.scalar.activation(su[s][1][:, lo:lo + TOK], src, ACT.Square,
                                                        bias=col_1[:, c:c + 1])
                        last.then_inc(by_act[s].sem, 1)
                    elif kind == "GE":
                        m = step[2]
                        part = su[s][1][:, m * 512:(m + 1) * 512]
                        wait(act, cubic, ("H", s, m), tile)
                        nc.scalar.activation(part, part, ACT.Tanh, scale=0.7978845608028654).then_inc(tanhed[s].sem, 1)

            take("head", 0)
            with act.Fori(1, turns) as it:
                take("body", it)
            take("tail", turns)

        @block.gpsimd
        def _(pool):
            chain = [0]

            def pre(ins):
                chain[0] += 1
                ins.then_inc(s_prepool, 1)
                pool.wait_ge(s_prepool, chain[0])

            pre(pool.memset(ident[:], 0.0))
            pre(pool.affine_select(out=ident[:], in_=ident[:], compare_op=ALU.not_equal, fill=1.0, base=0,
                                   pattern=[[-1, P]], channel_multiplier=1))
            pre(pool.memset(ones1[:], 1.0))
            pre(pool.memset(neghalf[:], -0.5))
            for g in (2, 4):
                w = 32 // g
                m = onehot[g]
                pre(pool.memset(m[:], 1.0))
                pre(pool.affine_select(out=m[:], in_=m[:], compare_op=ALU.is_ge, fill=0.0, base=0,
                                       pattern=[[-32, 4], [-w, g]], channel_multiplier=1))
                pre(pool.affine_select(out=m[:], in_=m[:], compare_op=ALU.is_ge, fill=0.0, base=w - 1,
                                       pattern=[[32, 4], [w, g]], channel_multiplier=-1))
            pool.sem_inc(s_const, 1)
            credit(pool, offset, scaled, biased, offmask, finished, pool_link)
            pool.wait_ge(s_prep, DVE_READY)

            def take(section, it):
                for n_step, (step, lag) in enumerate(SECTIONS[section]):
                    kind, s, tile = step[0], step[1], it - lag if lag else it
                    links = [0]

                    def link(ins):
                        one = pool_link[s]
                        ins.then_inc(one.sem, 1)
                        pool.wait_ge(one.sem, one.now((step, links[0]), tile))
                        links[0] += 1

                    if kind == "XB":
                        a = step[2]
                        bias = row_o[a][:, :].unsqueeze(1).to_broadcast([P, SUB, D])
                        if a == "S":
                            wait(pool, x_loaded, ("tile", s), tile)
                            wait_before(pool, by_dve, (("OP", s, "G"), "out"), tile)
                        else:
                            made = {"C": ("OP", s, "S"), "M": ("OP", s, "C"), "G": ("Y", s)}[a]
                            wait(pool, by_dve, (made, "out"), tile)
                        pool.tensor_tensor(xb[s][:], (xin[s][:] if a == "S" else xr[s][:]), bias,
                                           ALU.add).then_inc(biased[s].sem, 1)
                        if a == "S":
                            wait(pool, mc_loaded, ("tile", s), tile)
                            stand(pool)
                            pool.tensor_scalar(off_c[s][:], mask_c[s][:], -1.0, 10000.0, ALU.add,
                                               ALU.mult).then_inc(offmask[s].sem, 1)
                    elif kind == "ST":
                        wait(pool, moments, step, tile)
                        stand(pool)
                        link(pool.tensor_scalar(veps[s][:], mv[s][:, :, 1], EPS[step[2]], 1.0, ALU.add, ALU.mult))
                        pool.tensor_tensor(rstd[s][:], veps[s][:], neghalf[:], ALU.pow).then_inc(scaled[s].sem, 1)
                    elif kind == "FN":
                        wait(pool, normed, step, tile)
                        link(pool.tensor_tensor(res[s][:], res[s][:],
                                                gamma[:, :].unsqueeze(1).to_broadcast([P, SUB, D]), ALU.mult))
                        pool.tensor_tensor(res[s][:], res[s][:], beta[:, :].unsqueeze(1).to_broadcast([P, SUB, D]),
                                           ALU.add).then_inc(finished[s].sem, 1)
                    elif kind == "SC" and step[2] != "G":
                        a, t = step[2:]
                        off = off_s[:, :] if a == "S" else off_c[s][:, t]
                        if a == "C":
                            wait(pool, offmask, ("tile", s), tile)
                        wait(pool, masked, step, tile)
                        v = su_view(s, a, t).rearrange("p (h k) -> p h k", k=SEQ)
                        pool.tensor_tensor(v, v, off.unsqueeze(1).to_broadcast([P, HEADS[a], SEQ]),
                                           ALU.add).then_inc(offset[s].sem, 1)

            take("head", 0)
            with pool.Fori(1, turns) as it:
                take("body", it)
            take("tail", turns)

        @block.vector
        def _(dve):
            chain = [0]

            def pre(ins):
                chain[0] += 1
                ins.then_inc(s_pre, 1)
                dve.wait_ge(s_pre, chain[0])

            for s in both:
                for key, a in (("L", "S"), ("G", "G")):
                    v, w = vb[key][s], HD[a] + 1
                    pre(dve.memset(v[:], 0.0))
                    for j in range(2):
                        pre(dve.memset(v[64 * j:64 * j + 64, :, :, w * j + w - 1:w * j + w], 1.0))
                    c = vcross[key][s]
                    pre(dve.memset(c[:], 0.0))
                    for j in range(2):
                        pre(dve.memset(c[64 - 64 * j:P - 64 * j, :, :, w * j + w - 1:w * j + w], 1.0))
            dve.wait_ge(s_rows, 16 * 4)
            for row, stored_row in ((row_k, row_kn), (row_v["G"], row_vn)):
                pre(dve.tensor_copy(row[0:1, :].rearrange("p (h g d) -> p h g d", g=4, d=8),
                                    stored_row[0:1, :].rearrange("p (h d) -> p h d", d=8).unsqueeze(2)
                                    .to_broadcast([1, 8, 4, 8])))
            dve.wait_ge(s_const, 1)
            dve.wait_ge(s_prepool, 10)
            for g in (2, 4):
                pre(dve.tensor_reduce(headmask[g][:], onehot[g][:].rearrange("p i j -> p j i"), AX.X, ALU.add))
            dve.sem_inc(s_prep, 1)
            dve.wait_ge(s_turned, 1)
            pre(dve.tensor_copy(col_k["G"][:], ring[0][:, 0:KC]))
            dve.wait_ge(s_turned, 2)
            for n, a in enumerate("SCG"):
                pre(dve.tensor_copy(vspread[a][:].rearrange("p k n -> p (k n)"), ring[1 + n][:, 0:KC * P]))
            dve.sem_inc(s_prep, 1)
            dve.wait_ge(s_small, small)
            pre(dve.tensor_scalar(off_s[:], mask_s[:], -1.0, 10000.0, ALU.add, ALU.mult))
            for a in "SCG":
                pre(dve.tensor_scalar(col_q[a][:], col_q[a][:], HD[a] ** -0.5, None, ALU.mult))
            for a in "SCG":
                pre(dve.tensor_tensor(kmask[a][:], col_k[a][:, :].unsqueeze(2).to_broadcast([P, KC, JOINT[a]]),
                                      headmask[JOINT[a]][:, :].unsqueeze(1).to_broadcast([P, KC, JOINT[a]]), ALU.mult))
            dve.wait_ge(s_turned, 3)
            for n, a in enumerate("SCG"):
                pre(dve.tensor_tensor(row_o[a][:], row_o[a][:], scores[:, n, 0:D], ALU.add))
            dve.wait_ge(s_wrest, 16 * 7)
            for k in range(KC):
                pre(dve.tensor_copy(g_k[:, k, :].rearrange("p (h g d) -> p h g d", g=4, d=8),
                                    g_kn[:, k, :].rearrange("p (h d) -> p h d", d=8).unsqueeze(2)
                                    .to_broadcast([P, 8, 4, 8])))
            dve.sem_inc(s_prep, 1)
            credit(dve, by_dve, masked, shifted, moments, normed, cubic, gelued, dve_link)

            def take(section, it):
                for n_step, (step, lag) in enumerate(SECTIONS[section]):
                    kind, s, tile = step[0], step[1], it - lag if lag else it
                    links = [0]

                    def link(ins):
                        one = dve_link[s]
                        ins.then_inc(one.sem, 1)
                        dve.wait_ge(one.sem, one.now((step, links[0]), tile))
                        links[0] += 1

                    if kind == "ST":
                        if step[2] == 1:
                            wait(dve, x_loaded, ("tile", s), tile)
                        src = xin[s] if step[2] == 1 else xr[s]
                        for t in range(SUB):
                            last = dve.bn_stats(stats[s][:, t, :], src[:, t, :])
                        link(last)
                        stand(dve)
                        for t in range(SUB):
                            last = dve.bn_aggr(mv[s][:, t, :], stats[s][:, t, :])
                        last.then_inc(moments[s].sem, 1)
                    elif kind in ("LN", "FN"):
                        n = 4 if kind == "FN" else step[2]
                        src, dst = (xin[s] if n == 1 else xr[s]), (res[s] if n == 4 else z[s])
                        wait(dve, scaled, ("ST", s, n), tile)
                        if n == 4:
                            wait_before(dve, stored, ("tile", s), tile)
                        for t in range(SUB):
                            last = dve.tensor_scalar(dst[:, t, :], src[:, t, :], mv[s][:, t, 0:1],
                                                     rstd[s][:, t:t + 1], ALU.subtract, ALU.mult)
                        last.then_inc(normed[s].sem, 1)
                    elif kind == "SC":
                        a, t = step[2:]
                        m = {"S": mask_s[:, :], "C": mask_c[s][:, t], "G": mask_g[s][:, t]}[a]
                        if a == "C":
                            wait(dve, mc_loaded, ("tile", s), tile)
                        if a == "G":
                            wait(dve, mg_loaded, ("tile", s), tile)
                        wait(dve, scored, step, tile)
                        h = HEADS[a] // 4
                        dve.tensor_tensor(su_view(s, a, t).rearrange("p (i h k) -> p i h k", i=4, k=SEQ), score_view(a),
                                          m.unsqueeze(1).unsqueeze(1).to_broadcast([P, 4, h, SEQ]),
                                          ALU.add if a == "G" else ALU.mult).then_inc(masked[s].sem, 1)
                    elif kind == "MX":
                        a, t = step[2:]
                        if a == "G":
                            wait(dve, masked, ("SC", *step[1:]), tile)
                        else:
                            wait(dve, offset, ("SC", *step[1:]), tile)
                        v = su_view(s, a, t).rearrange("p (h k) -> p h k", k=SEQ)
                        top = mx[s][:, t, 0:HEADS[a]]
                        link(dve.tensor_reduce(top, v, AX.X, ALU.max))
                        dve.tensor_tensor(v, v, top.unsqueeze(2).to_broadcast([P, HEADS[a], SEQ]),
                                          ALU.subtract).then_inc(shifted[s].sem, 1)
                    elif kind == "PO":
                        a, t = step[2:]
                        n, w = HEADS[a], HD[a] + 1
                        wait(dve, filled, (step, "o"), tile)
                        o = bank(step, "o")[:, 0:n * w].rearrange("p (h d) -> p h d", d=w)
                        link(dve.reciprocal(rden[s][:, t, 0:n], o[:, :, w - 1]))
                        dve.tensor_tensor(attn_rows[s][:, t, :].rearrange("p (h d) -> p h d", d=w - 1), o[:, :, 0:w - 1],
                                          rden[s][:, t, 0:n].unsqueeze(2).to_broadcast([P, n, w - 1]),
                                          ALU.mult).then_inc(by_dve[s].sem, 1)
                    elif kind == "OP":
                        wait(dve, biased, ("XB", *step[1:]), tile)
                        wait(dve, filled, (step, "out"), tile)
                        dve.tensor_tensor(xr[s][:].rearrange("p t d -> p (t d)"), bank(step, "out")[:],
                                          xb[s][:].rearrange("p t d -> p (t d)"), ALU.add).then_inc(by_dve[s].sem, 1)
                        wait(dve, by_dve, (step, "out"), tile)
                    elif kind == "Y":
                        wait(dve, biased, ("XB", s, "M"), tile)
                        wait(dve, filled, (step, "out"), tile)
                        dve.scalar_tensor_tensor(out=xr[s][:].rearrange("p t d -> p (t d)"),
                                                 in0=bank(step, "out")[:], scalar=0.5,
                                                 in1=xb[s][:].rearrange("p t d -> p (t d)"), op0=ALU.mult,
                                                 op1=ALU.add).then_inc(by_dve[s].sem, 1)
                    elif kind == "H":
                        m = step[2]
                        hid, sq = su[s][0][:, m * 512:(m + 1) * 512], su[s][1][:, m * 512:(m + 1) * 512]
                        wait(dve, by_act, (step, "h"), tile)
                        link(dve.tensor_scalar(sq, sq, 0.044715, 1.0, ALU.mult, ALU.add))
                        dve.tensor_tensor(sq, sq, hid, ALU.mult).then_inc(cubic[s].sem, 1)
                    elif kind == "GE":
                        m = step[2]
                        hid, th = su[s][0][:, m * 512:(m + 1) * 512], su[s][1][:, m * 512:(m + 1) * 512]
                        wait(dve, tanhed, step, tile)
                        dve.scalar_tensor_tensor(out=hid, in0=th, scalar=1.0, in1=hid, op0=ALU.add,
                                                 op1=ALU.mult).then_inc(gelued[s].sem, 1)

            take("head", 0)
            with dve.Fori(1, turns) as it:
                take("body", it)
            take("tail", turns)

        @block.tensor
        def _(pe):
            pe.wait_ge(s_prep, 1)
            for k in range(KC):
                last = nc.tensor.matmul(ring[0][:, k:k + 1], row_k[0:1, k * P:(k + 1) * P], ones1[0:1, 0:1],
                                        start=True, stop=True)
            last.then_inc(s_turned, 1)
            for n, a in enumerate("SCG"):
                for k in range(KC):
                    last = nc.tensor.matmul(ring[1 + n][:, k * P:(k + 1) * P], row_v[a][0:1, k * P:(k + 1) * P],
                                            ones1[0:1, :], start=True, stop=True)
            last.then_inc(s_turned, 1)
            pe.wait_ge(s_prep, 2)
            pe.wait_ge(s_w1st, 16 * 4)
            for n, a in enumerate("SCG"):
                for k in range(KC):
                    last = nc.tensor.matmul(scores[:, n, 0:D], vspread[a][:, k, :], w_of[a][3][:, k, :],
                                            start=(k == 0), stop=(k == KC - 1))
            last.then_inc(s_turned, 1)
            pe.wait_ge(s_wrest, 16 * 7)
            pe.wait_ge(s_prep, DVE_READY)
            credit(pe, filled, scored)

            def claim(section, n_step, job, it, known=None):
                step, lag = SECTIONS[section][n_step]
                n = [u[:2] for u in JOBS[section]].index((step, job))
                user, back = last_user(JOBS, section, n, lambda u: BANK[u[:2]] == BANK[(step, job)])
                if user:
                    signal, ago = (by_act if user[3] == "act" else by_dve), user[2] + back
                    if known and known[0] is signal and user[0][1] == step[1]:
                        events = signal[step[1]].events
                        if ago > lag or events.index(user[:2]) <= events.index(known[1]):
                            return bank(step, job)
                        stand(pe)
                    wait(pe, signal, user[:2], it - ago if ago else it)
                return bank(step, job)

            def turn_rows(step, src, b):
                s = step[1]
                for k in range(KC):
                    for t in range(SUB):
                        last = nc.tensor.transpose(b[:, k * TOK + t * P:k * TOK + (t + 1) * P],
                                                   src[:, t, k * P:(k + 1) * P], ident[:])
                last.then_inc(filled[s].sem, 1)

            def project_cols(step, b, w, src, m0=0):
                s = step[1]
                for m in range(2):
                    for k in range(KC):
                        last = nc.tensor.matmul(b[:, m * TOK:(m + 1) * TOK], w[:, k, (m0 + m) * P:(m0 + m + 1) * P],
                                                src[:, k, :], start=(k == 0), stop=(k == KC - 1))
                last.then_inc(filled[s].sem, 1)

            def score_chunk(a, s, t, k):
                g = JOINT[a]
                for flip in range(2):
                    for i in range(4):
                        b = (i + flip) % 2
                        r, tok = slice(32 * i, 32 * i + 32), t * P + b * SEQ
                        dst = scores[64 * b:64 * b + 64, i, k * g * SEQ:(k + 1) * g * SEQ]
                        last = nc.tensor.matmul(dst.rearrange("p (j k) -> p j k", k=SEQ),
                                                qT[s][r, k, tok:tok + SEQ], kbd[s][r, k, 0:g, tok:tok + SEQ],
                                                start=True, stop=True)
                return last

            def take(section, it):
                for n_step, (step, lag) in enumerate(SECTIONS[section]):
                    kind, s, tile = step[0], step[1], it - lag if lag else it
                    if kind == "ET":
                        wait(pe, e_loaded, ("tile", s), tile)
                        turn_rows(step, ein[s], claim(section, n_step, "turn", it))
                    elif kind == "LN":
                        wait(pe, normed, step, tile)
                        turn_rows(step, z[s], claim(section, n_step, "turn", it))
                    elif kind == "XT":
                        known = by_dve, (("Y", s), "out")
                        wait(pe, *known, tile)
                        turn_rows(step, xr[s], claim(section, n_step, "turn", it, known))
                    elif kind == "CT":
                        known = by_dve, latest(by_dve, [(("PO", s, step[2], t), "o") for t in range(SUB)])
                        wait(pe, *known, tile)
                        turn_rows(step, attn_rows[s], claim(section, n_step, "turn", it, known))
                    elif kind == "QP":
                        a = step[2]
                        known = by_act, ({"S": ("LN", s, 1), "C": ("LN", s, 2), "G": ("XT", s)}[a], "turn")
                        wait(pe, *known, tile)
                        project_cols(step, claim(section, n_step, "proj", it, known), w_of[a][0], zT[s])
                    elif kind == "KP":
                        a = step[2]
                        known = by_act, (("LN", s, 1) if a == "S" else ("ET", s), "turn")
                        wait(pe, *known, tile)
                        project_cols(step, claim(section, n_step, "proj", it, known), w_of[a][1], zT[s] if a == "S" else eT[s])
                    elif kind == "V":
                        a = step[2]
                        src, w, width = (zT[s] if a == "S" else eT[s]), w_of[a][2], (64 if a == "G" else D)
                        known = by_act, (("LN", s, 1) if a == "S" else ("ET", s), "turn")
                        wait(pe, *known, tile)
                        b = claim(section, n_step, "v", it, known)
                        for t in range(SUB):
                            for k in range(KC):
                                last = nc.tensor.matmul(b[:, t * width:(t + 1) * width], src[:, k, t * P:(t + 1) * P],
                                                        w[:, k, :], start=(k == 0), stop=(k == KC - 1))
                        last.then_inc(filled[s].sem, 1)
                    elif kind == "SA":
                        a, t = step[2:]
                        wait(pe, by_act, latest(by_act, [(("QP", s, a), "proj"), (("KP", s, a), "proj")]), tile)
                        n = [u[0] for u in SCORES[section]].index(("SC", *step[1:]))
                        user, back = last_user(SCORES, section, n, lambda u: True)
                        if user:
                            ago = user[1] + back
                            wait(pe, masked, user[0], it - ago if ago else it)
                        score_chunk(a, s, t, 0)
                    elif kind == "SC":
                        a, t = step[2:]
                        score_chunk(a, s, t, 1).then_inc(scored[s].sem, 1)
                    elif kind == "PT":
                        a, t = step[2:]
                        wait(pe, probs, ("MX", *step[1:]), tile)
                        for n in range(PT_JOBS[a]):
                            b = claim(section, n_step, f"p{n}", it)
                            for c in range(4):
                                lo = (4 * n + c) * P
                                last = nc.tensor.transpose(b[:, c * P:(c + 1) * P], su[s][t][:, lo:lo + P], ident[:])
                            last.then_inc(filled[s].sem, 1)
                    elif kind == "PO":
                        wait(pe, crossed[cross(step[2])], ("V", s, step[2]), tile)
                        stand(pe)
                        a, t = step[2:]
                        known = by_act, latest(by_act, [(("PT", *step[1:]), f"p{PT_JOBS[a] - 1}"),
                                                        (("V", s, a), "v")])
                        wait(pe, *known, tile)
                        b = claim(section, n_step, "o", it, known)
                        g2, w = JOINT[a] // 2, PAIRW[a]
                        for pair in range(PAIRS[a]):
                            i, k, jj = pair // (KC * g2), pair // g2 % KC, pair % g2
                            group = 4 * k + i
                            at = (group * g2 + jj) * w
                            for q in range(BPS):
                                last = nc.tensor.matmul(b[64 * q:64 * q + 64, at:at + w],
                                                        pT[s][:, pair * P + q * SEQ:pair * P + (q + 1) * SEQ],
                                                        vb[cross(a)][s][:, t * BPS + q, group, :], start=True, stop=True)
                        last.then_inc(filled[s].sem, 1)
                    elif kind == "OP":
                        known = by_act, (("CT", *step[1:]), "turn")
                        wait(pe, *known, tile)
                        b = claim(section, n_step, "out", it, known)
                        for t in range(SUB):
                            for k in range(KC):
                                last = nc.tensor.matmul(b[:, t * D:(t + 1) * D], cT[s][:, k, t * P:(t + 1) * P],
                                                        w_of[step[2]][3][:, k, :], start=(k == 0), stop=(k == KC - 1))
                        last.then_inc(filled[s].sem, 1)
                    elif kind == "H":
                        known = by_act, (("LN", s, 3), "turn")
                        wait(pe, *known, tile)
                        project_cols(step, claim(section, n_step, "h", it, known), w_1, zT[s], 2 * step[2])
                    elif kind == "Y":
                        wait(pe, gelued, latest(gelued, [("GE", s, m) for m in range(HC // 2)]), tile)
                        b = claim(section, n_step, "out", it)
                        for t in range(SUB):
                            for m in range(HC):
                                lo = m * TOK + t * P
                                last = nc.tensor.matmul(b[:, t * D:(t + 1) * D], su[s][0][:, lo:lo + P], w_2[:, m, :],
                                                        start=(m == 0), stop=(m == HC - 1))
                        last.then_inc(filled[s].sem, 1)

            take("head", 0)
            with pe.Fori(1, turns) as it:
                take("body", it)
            take("tail", turns)


NAMES = {"x": "x", "ctx": "ctx_2048", "mask_s": "mask_1x1xSxS2_fc1", "mask_c": "mask_Bx1xSxS2_ff1",
         "mask_g": "mask_Bx1xSxS2_ff0",
         **{n: f"L0_xattn_{n}" for n in ("ln1_s", "ln1_b", "w_qkv", "b_qkv", "w_ao", "b_ao", "ln2_s", "ln2_b", "w_q",
                                         "b_q", "w_kv", "b_kv", "w_co", "b_co", "ln3_s", "ln3_b", "b1", "b2")},
         "w_1": "L0_xattn_w1", "w_2": "L0_xattn_w2",
         **{n: f"L1_xattn_{n}" for n in ("Wq", "bq", "Wk", "bk", "Wv", "bv", "Wo", "bo", "gamma", "beta")}}


def kernel(**inputs):
    import numpy as np
    import concourse.bacc as bacc
    from concourse.bass_utils import run_bass_kernel_spmd as run

    nc = bacc.Bacc("TRN2", target_bir_lowering=False, num_devices=1)
    arrays, io = {}, {}
    for short, name in NAMES.items():
        a = np.ascontiguousarray(inputs[name])
        arrays[f"in_{name}"] = a
        io[short] = nc.dram_tensor(f"in_{name}", a.shape, mybir.dt.from_np(a.dtype), kind="ExternalInput").ap()
    out = nc.dram_tensor("out_0", inputs["x"].shape, F32, kind="ExternalOutput").ap()
    build(nc, io, out)
    r = run(nc, [arrays], core_ids=[0])
    return r.results[0]["out_0"]
```
